# Optimizing a Trainium2 kernel written in Bass

```python
import numpy as np
import jax
import jax.numpy as jnp

def _softmax(x, axis=-1):
    return jax.nn.softmax(x, axis=axis)

def _gelu(x):
    return jax.nn.gelu(x, approximate=True)

def _silu(x):
    return jax.nn.silu(x)

def _sigmoid(x):
    return jax.nn.sigmoid(x)

def _layernorm(x, axis=-1, eps=1e-05):
    m = jnp.mean(x, axis=axis, keepdims=True)
    v = jnp.var(x, axis=axis, keepdims=True)
    return (x - m) / jnp.sqrt(v + eps)

def _scatter_add(tgt, idx, src, axis=0):
    return tgt.at[idx].add(src)

def _segment_sum(src, seg, n):
    return jax.ops.segment_sum(src, seg, n)
kernel_name = 'mk_gnn_resnorm_d2_gnn_r32_95b544'

def setup_inputs(seed: int=0):
    np.random.seed(seed)
    _w = jnp.asarray

    def _rec_inputs():
        import jax
        import jax.numpy as jnp
        _gk = jax.random.key(seed)
        x = -0.0005121 + 1.001 * jax.random.normal(jax.random.fold_in(_gk, 1), (50000, 64), jnp.float32)
        _s = jax.random.randint(jax.random.fold_in(_gk, 2), (25000,), 0, 50000, jnp.int32)
        _d = jax.random.randint(jax.random.fold_in(_gk, 3), (25000,), 0, 50000, jnp.int32)
        _loop = jnp.arange(50000, dtype=jnp.int32)
        src = jnp.concatenate([_s, _d, _loop])
        dst = jnp.concatenate([_d, _s, _loop])
        _o = jnp.argsort(dst, stable=True)
        src = src[_o]
        dst = dst[_o]
        return (x, src, dst)
    x, src, dst = _rec_inputs()

    def _L0_gnn_setup():
        import jax, jax.numpy as jnp
        import numpy as np
        N_NODES = 50000
        N_EDGES = 25000
        IN_CH = 64
        HID = 128
        OUT_CH = 64
        BN_EPS = 1e-05
        key = jax.random.key(seed)
        k = jax.random.split(key, 6)
        x = jax.random.normal(k[0], (N_NODES, IN_CH), dtype=jnp.float32)
        edge_index = jax.random.randint(k[1], (2, N_EDGES), 0, N_NODES, dtype=jnp.int64)
        gamma = jnp.ones((IN_CH,), dtype=jnp.float32)
        beta = jnp.zeros((IN_CH,), dtype=jnp.float32)
        W1 = jax.random.normal(k[2], (2 * IN_CH, HID), dtype=jnp.float32) * 0.05
        b1 = jnp.zeros((HID,), dtype=jnp.float32)
        W2 = jax.random.normal(k[3], (HID, OUT_CH), dtype=jnp.float32) * 0.05
        b2 = jnp.zeros((OUT_CH,), dtype=jnp.float32)
        return {'x': x, 'edge_index': edge_index, 'gamma': gamma, 'beta': beta, 'W1': W1, 'b1': b1, 'W2': W2, 'b2': b2}
    _L0_gnn_all = _L0_gnn_setup()
    _L0_gnn_in = {k: v for k, v in _L0_gnn_all.items() if k in ('gamma', 'beta', 'W1', 'b1', 'W2', 'b2')}
    del _L0_gnn_all

    def _L1_gnn_setup():
        import jax, jax.numpy as jnp
        import numpy as np
        N_NODES = 50000
        N_EDGES = 31250
        D_IN = 64
        D_OUT = 64
        key = jax.random.key(seed)
        kx, ks, kd, ku, kv = jax.random.split(key, 5)
        x = jax.random.normal(kx, (N_NODES, D_IN), dtype=jnp.float32)
        src = jax.random.randint(ks, (N_EDGES,), 0, N_NODES)
        dst = jax.random.randint(kd, (N_EDGES,), 0, N_NODES)
        std = float(np.sqrt(2.0 / (D_IN + D_OUT)))
        U = jax.random.normal(ku, (D_OUT, D_IN), dtype=jnp.float32) * std
        V = jax.random.normal(kv, (D_OUT, D_IN), dtype=jnp.float32) * std
        return {'x': x, 'src': src, 'dst': dst, 'U': U, 'V': V}
    _L1_gnn_all = _L1_gnn_setup()
    _L1_gnn_in = {k: v for k, v in _L1_gnn_all.items() if k in ('U', 'V')}
    del _L1_gnn_all
    return {'x': x, 'src': src, 'dst': dst, 'L0_gnn_gamma': _L0_gnn_in['gamma'], 'L0_gnn_beta': _L0_gnn_in['beta'], 'L0_gnn_W1': _L0_gnn_in['W1'], 'L0_gnn_b1': _L0_gnn_in['b1'], 'L0_gnn_W2': _L0_gnn_in['W2'], 'L0_gnn_b2': _L0_gnn_in['b2'], 'L1_gnn_U': _L1_gnn_in['U'], 'L1_gnn_V': _L1_gnn_in['V']}

def reference(x, src, dst, L0_gnn_gamma, L0_gnn_beta, L0_gnn_W1, L0_gnn_b1, L0_gnn_W2, L0_gnn_b2, L1_gnn_U, L1_gnn_V):
    import jax
    import jax.numpy as jnp

    def _L0_gnn_ref(x, edge_index, gamma, beta, W1, b1, W2, b2):
        import jax, jax.numpy as jnp
        import numpy as np
        N_NODES = 50000
        N_EDGES = 25000
        IN_CH = 64
        HID = 128
        OUT_CH = 64
        BN_EPS = 1e-05
        mean = jnp.mean(x, axis=0)
        var = jnp.mean(jnp.square(x - mean), axis=0)
        xn = (x - mean) * jax.lax.rsqrt(var + BN_EPS) * gamma + beta
        src = edge_index[0]
        dst = edge_index[1]
        xi = xn[dst]
        xj = xn[src]
        feat = jnp.concatenate([xi, xj - xi], axis=-1)
        h = jax.nn.relu(feat @ W1 + b1)
        msg = h @ W2 + b2
        agg = jax.ops.segment_max(msg, dst, num_segments=N_NODES)
        agg = jnp.where(jnp.isfinite(agg), agg, 0.0)
        return jax.nn.relu(agg)

    def _L1_gnn_ref(x, src, dst, U, V):
        import jax, jax.numpy as jnp
        import numpy as np
        N_NODES = 50000
        N_EDGES = 31250
        D_IN = 64
        D_OUT = 64
        agg = jax.ops.segment_sum(x[src], dst, num_segments=x.shape[0])
        out = jax.nn.relu(jnp.einsum('nd,od->no', x, U) + jnp.einsum('nd,od->no', agg, V))
        return out
    edge_index = jnp.stack([src, dst])
    x = _layernorm(x + _L0_gnn_ref(x, edge_index, L0_gnn_gamma, L0_gnn_beta, L0_gnn_W1, L0_gnn_b1, L0_gnn_W2, L0_gnn_b2), axis=-1)
    x = _layernorm(x + _L1_gnn_ref(x, src, dst, L1_gnn_U, L1_gnn_V), axis=-1)
    return x

_drawn_inputs = setup_inputs


def setup_inputs(seed=0):
    import zlib

    import numpy as np

    out = dict(_drawn_inputs(seed))
    spreads = {'L0_gnn_gamma': (1.0, 0.2),
     'L0_gnn_beta': (0.0, 0.47),
     'L0_gnn_b1': (0.0, 0.1),
     'L0_gnn_b2': (0.0, 0.1)}
    factors = {}
    for name, (base, spread) in spreads.items():
        noise = np.random.default_rng([zlib.crc32(name.encode()), seed]).standard_normal(out[name].shape)
        drawn = base * np.exp(spread * noise) if base else spread * noise
        out[name] = jnp.asarray(drawn.astype(out[name].dtype))
    for name, factor in factors.items():
        out[name] = (out[name] * factor).astype(out[name].dtype)
    return out
```

```python
import concourse.bass as bass
from concourse import mybir
from contextlib import ExitStack

F32 = mybir.dt.float32
BF16 = mybir.dt.bfloat16
I32 = mybir.dt.int32
ALU = mybir.AluOpType
ACT = mybir.ActivationFunctionType
AX = mybir.AxisListType

N = 50000
E = 100000
C = 64
HID = 128
P = 128
EPS = 1e-5

S = 4
GE = S * P
U = 4
G = U * -(-E // (U * GE))
T = G * S
EP = G * GE
IDX_COLS = T + U * S

MW = P // 2 + 1
D = 4
DM = D * P
K = -(-(N // 2) // DM)
MP = K * DM
NP = 2 * MP

XR = N // P
XT = N - XR * P
XC = 5
XRC = XR // XC
XB = 6
XN = XRC // XB
assert XC * XRC == XR and XB * XN == XRC

BIG = 3.0e38


def reused(g):
    return not isinstance(g, int) or g >= 2


def gnn_kernel(nc, x, src_cols, dst_cols, dst_prev_cols, dst_next_cols, dst_rows, dst_prev_rows, dst_low,
               gamma, beta, W1, b1, W2, b2, U_t, V_t, out):
    y_dram = nc.dram_tensor("y_dram", [MP, 2 * C], F32, kind="Internal").ap()
    mask_dram = nc.dram_tensor("mask_dram", [2, EP], BF16, kind="Internal").ap()

    ctx = ExitStack()
    with ctx:
        def sb(name, shape, dt=F32):
            return ctx.enter_context(nc.sbuf_tensor(name, shape, dt))

        def sem(name):
            return ctx.enter_context(nc.semaphore(name))

        agg = sb("agg", [P, MP])
        ident = sb("ident", [P, P])
        ones = sb("ones", [P, P])
        iota_i = sb("iota_i", [P, 2 * MW], I32)
        dcol = sb("dcol", [P, T], I32)
        dprev = sb("dprev", [P, T], I32)
        dnext = sb("dnext", [P, T], I32)
        mb = sb("mb", [P, T], I32)
        mb2 = sb("mb2", [P, T], I32)
        first = sb("first", [P, T])
        rel = sb("rel", [P, T])
        rel_end = sb("rel_end", [P, T])
        carry_row = sb("carry_row", [P, T], BF16)
        reset_row = sb("reset_row", [P, T], BF16)
        wb = sb("wb", [P, HID])
        wa = sb("wa", [P, HID])
        wh = sb("wh", [P, HID])
        w2 = sb("w2", [HID, C])
        b1c = sb("b1c", [P, 1])
        b1f = sb("b1f", [P, 1])
        b2c = sb("b2c", [P, 1])
        gam = sb("gam", [P, 1])
        bet = sb("bet", [P, 1])
        bdu = sb("bdu", [P, P])
        bdv = sb("bdv", [P, P])
        statrow = sb("statrow", [P, 2, 2, C])
        cols = sb("cols", [P, 8])
        epsc = sb("epsc", [P, 1])
        zero = sb("zero", [P, 1])
        half = sb("half", [P, 2 * D])
        idx = [sb(f"idx{h}", [P, 2 * S], I32) for h in range(2)]
        xx = [sb(f"xx{u}", [P, S, 2 * C]) for u in range(U)]
        xsxd = [sb(f"xsxd{u}", [P, GE]) for u in range(U)]
        masks = [sb(f"masks{u}", [P, GE], BF16) for u in range(U)]
        hid = [sb(f"hid{i}", [P, GE]) for i in range(2)]
        runmax = [sb(f"runmax{i}", [P, GE]) for i in range(2)]
        mrow = sb("mrow", [P, S, C])
        onehot = [sb(f"onehot{i}", [P, S, 2 * MW]) for i in range(2)]
        xt = [hid[i] for i in range(2)] + [sb(f"xt{i}", [P, DM]) for i in range(2)]
        act_t = [xsxd[i] for i in range(2)]
        y_t = [xsxd[2 + i] for i in range(2)]
        cen = [sb(f"cen{i}", [P, DM]) for i in range(2)]
        sq = [sb(f"sq{i}", [P, DM]) for i in range(2)]
        res = [sb(f"res{i}", [P, DM]) for i in range(2)]
        ssum = sb("ssum", [P, 2, 2 * D])
        nmean = sb("nmean", [P, 2, 2 * D])
        ssq = sb("ssq", [P, 2, 2 * D])
        var = sb("var", [P, 2, 2 * D])
        rstd = sb("rstd", [P, 2, 2 * D])

        bank = [ctx.enter_context(nc.psum_tensor(f"bank{i}", [P, 512], F32)) for i in range(8)]
        ps_xt = bank[0:2]
        ps_h = bank[2:4]
        ps_m = bank[4:6]
        ps_bt = bank[6][:, :].rearrange("p (s c) -> p s c", s=S)
        ps_sel = bank[7][:, 0:S * MW].rearrange("p (s m) -> p s m", s=S)
        iota_p = bank[7][:, 320:320 + 2 * MW]
        ps_sum, ps_ssq, ps_mean, ps_cols = bank[2], bank[3], bank[4][:, 0:C], bank[5]

        s_xl = [sem(f"x_loaded{c}") for c in range(XC + 1)]
        s_edges = sem("edge_tables_loaded")
        s_weights = sem("weights_loaded")
        s_pool = sem("pool_constants")
        s_const = sem("dve_constants")
        s_wu = sem("weights_uv_loaded")
        s_tab = sem("tables_step")
        s_maskrows = sem("mask_rows_stored")
        s_sum = sem("x_summed")
        s_mean = sem("mean_ready")
        s_cen = sem("x_centred")
        s_sq = sem("x_squared")
        s_ssq = sem("squares_summed")
        s_st = sem("statistics_step")
        s_colp = sem("statistics_columns")
        s_std = sem("std_ready")
        s_bias = sem("bias_product")
        s_wready = sem("layer0_weights_ready")
        s_aggz = sem("agg_zeroed")
        s_idx = [sem(f"idx_loaded{h}") for h in range(2)]
        s_gather = [sem(f"gathered{u}") for u in range(U)]
        s_mask = [sem(f"masks_loaded{u}") for u in range(U)]
        s_clear = sem("gather_slots_clear")
        s_pre = sem("loop_rows_marked")
        s_t = sem("x_transposed")
        s_xs = sem("xs_copied")
        s_xd = sem("xd_scanned")
        s_h = sem("hidden_product")
        s_relu = sem("hidden_ready")
        s_m = sem("message_product")
        s_ms = sem("max_scanned")
        s_bt = sem("max_transposed")
        s_btc = sem("max_rows_copied")
        s_hot = sem("onehot_ready")
        s_sel = sem("windows_ready")
        s_add = sem("windows_added")
        s_idx1 = [sem(f"idx1_loaded{h}") for h in range(2)]
        s_gather1 = [sem(f"gathered1_{u}") for u in range(U)]
        s_hot1 = sem("onehot1_ready")
        s_sel1 = sem("windows1_ready")
        s_add1 = sem("windows1_added")

        class NodeSems:
            def __init__(self, tag):
                self.loaded = [sem(f"{tag}_rows_loaded{i}") for i in range(4)]
                self.y_t = sem(f"{tag}_rows_transposed")
                self.y_c = sem(f"{tag}_rows_transposed_copied")
                self.z = sem(f"{tag}_uv_product")
                self.act = sem(f"{tag}_relu")
                self.zero = sem(f"{tag}_agg_cleared")
                self.back = sem(f"{tag}_transposed")
                self.v = sem(f"{tag}_residual")
                self.sum = sem(f"{tag}_sum")
                self.nm = sem(f"{tag}_negmean")
                self.cen = sem(f"{tag}_centred")
                self.sq = sem(f"{tag}_squared")
                self.ssq = sem(f"{tag}_squares_summed")
                self.var = sem(f"{tag}_variance")
                self.rstd = sem(f"{tag}_rstd")
                self.res = sem(f"{tag}_normed")
                self.stored = [sem(f"{tag}_stored{i}") for i in range(2)]

        n0, n1 = NodeSems("n0"), NodeSems("n1")

        x_flat = x.rearrange("(m r) c -> m (r c)", r=2)
        x_nodes = x_flat.rearrange("(k p j) c -> k p (j c)", p=P, j=D)
        y_nodes = y_dram.rearrange("(k p j) c -> k p (j c)", p=P, j=D)
        out_nodes = out.rearrange("(m r) c -> m (r c)", r=2).rearrange("(k p j) c -> k p (j c)", p=P, j=D)
        y_rows = y_dram.rearrange("m (r c) -> (m r) c", r=2)
        x_stat = x[0:XR * P, :].rearrange("(p n) c -> p (n c)", p=P)
        xs_view = agg[:, 0:XR * C]
        x_tail = agg[0:XT, XR * C:XR * C + C]

        last0, last1 = G + 3, G + 1

        block = ctx.enter_context(nc.Block())

        @block.sync
        def _(sp):
            for h in range(2):
                sp.dma_start(idx[h][:, :], src_cols[:, 2 * S * h:2 * S * (h + 1)]).then_inc(s_idx[h], 16)
            for c in range(XC):
                sp.dma_start(xs_view[:, c * XRC * C:(c + 1) * XRC * C],
                             x_stat[:, c * XRC * C:(c + 1) * XRC * C]).then_inc(s_xl[c], 16)
            sp.dma_start(x_tail, x[XR * P:N, :]).then_inc(s_xl[XC], 16)
            sp.wait_ge(s_maskrows, 32)

            def load_masks(g, u, reuse):
                if reuse:
                    sp.wait_ge(s_ms, g - U + 1)
                for row, lo in ((1, 0), (0, C)):
                    sp.dma_start(masks[u][lo:lo + C, :],
                                 mask_dram[row:row + 1, bass.ds(g * GE, GE)].to_broadcast([C, GE])
                                 ).then_inc(s_mask[u], 16)

            def load_idx(it, h, gathered, loaded):
                for u in (2 * h, 2 * h + 1):
                    sp.wait_ge(gathered[u], it * S * 16 + S * 16)
                sp.dma_start(idx[h][:, :],
                             src_cols[:, bass.ds(it * (U * S) + (U * S + 2 * S * h), 2 * S)]).then_inc(loaded[h], 16)

            def body0(it, reuse):
                for h in range(2):
                    for u in (2 * h, 2 * h + 1):
                        load_masks(it * U + u, u, reuse)
                    load_idx(it, h, s_gather, s_idx)

            body0(0, False)
            with sp.Fori(1, G // U) as it:
                body0(it, True)

            def node_pass(ns, src, dst, lag):
                def step(k, u, load, reuse, store):
                    if load:
                        if reuse:
                            sp.wait_ge(ns.v, k - 3)
                        sp.dma_start(xt[u][:, :], src[bass.ds(k, 1), :, :].rearrange("k p c -> (k p) c")
                                     ).then_inc(ns.loaded[u], 16)
                    if store:
                        sp.wait_ge(ns.res, k - lag - 1)
                        sp.dma_start(dst[bass.ds(k - (lag + 2), 1), :, :].rearrange("k p c -> (k p) c"),
                                     res[(u - lag) % 2][:, :]).then_inc(ns.stored[(u - lag) % 2], 16)
                for k in range(U):
                    step(k, k, True, False, k - lag - 2 >= 0)
                with sp.Fori(1, K // U) as it:
                    for u in range(U):
                        step(it * U + u, u, True, True, True)
                for k in range(K // U * U, K + lag + 2):
                    step(k, k % U, k < K, True, True)
                for i in range(2):
                    sp.wait_ge(ns.stored[i], 16 * ((K + 1 - i) // 2))

            sp.wait_ge(s_m, G)
            node_pass(n0, x_nodes, y_nodes, 0)
            for h in range(2):
                sp.dma_start(idx[h][:, :], src_cols[:, 2 * S * h:2 * S * (h + 1)]).then_inc(s_idx1[h], 16)
            for h in range(2):
                load_idx(0, h, s_gather1, s_idx1)
            with sp.Fori(1, G // U) as it:
                for h in range(2):
                    load_idx(it, h, s_gather1, s_idx1)
            node_pass(n1, y_nodes, out_nodes, 1)
            for h in range(2):
                sp.wait_ge(s_idx[h], 16 * (G // U + 1))
                sp.wait_ge(s_idx1[h], 16 * (G // U + 1))

        @block.gpsimd
        def _(pool):
            pool.memset(ident[:, :], 0.0).then_inc(s_pool, 1)
            pool.memset(ones[:, :], 1.0).then_inc(s_pool, 1)
            pool.memset(half[:, :], -0.5).then_inc(s_pool, 1)
            pool.memset(zero[:, :], 0.0).then_inc(s_pool, 1)
            pool.memset(bdu[:, :], 0.0).then_inc(s_pool, 1)
            pool.memset(bdv[:, :], 0.0).then_inc(s_pool, 1)
            pool.iota(iota_i[:, :], pattern=[[1, 2], [2, MW]], base=0, channel_multiplier=0).then_inc(s_pool, 1)
            pool.wait_ge(s_pool, 7)
            pool.affine_select(out=ident[:, :], in_=ident[:, :], compare_op=ALU.not_equal, fill=1.0,
                               base=0, pattern=[[-1, P]], channel_multiplier=1).then_inc(s_pool, 1)

            def gather_group(it, u, table, loaded, gathered):
                h = u // 2
                if u % 2 == 0:
                    pool.wait_ge(loaded[h], it * 16 + 16)
                pool.sem_inc(s_clear, 1)
                for s in range(S):
                    col = (u % 2) * S + s
                    pool.indirect_dma_start(out=xx[u][:, s, 0:C], out_offset=None, in_=table,
                                            in_offset=bass.IndirectOffsetOnAxis(ap=idx[h][:, col:col + 1], axis=0),
                                            ).then_inc(gathered[u], 16)

            for u in range(U):
                gather_group(0, u, x, s_idx, s_gather)
            with pool.Fori(1, G // U) as it:
                for u in range(U):
                    pool.wait_ge(s_t, it * U + (u - U + 1))
                    gather_group(it, u, x, s_idx, s_gather)

            def node_pass(ns, lag, clear):
                def step(k, u, do_clear, norm, reuse):
                    if do_clear:
                        pool.wait_ge(ns.act, k + 1)
                        pool.tensor_copy(agg[:, bass.ds(k * DM, DM)], zero[:, :].to_broadcast([P, DM])
                                         ).then_inc(ns.zero, 1)
                    if norm:
                        i = (u - lag) % 2
                        pool.wait_ge(ns.var, k - lag - 1)
                        pool.tensor_tensor(rstd[:, i, :], var[:, i, :], half[:, :], ALU.pow).then_inc(ns.rstd, 1)
                        pool.wait_ge(ns.rstd, k - lag - 1)
                        if reuse is not None:
                            pool.wait_ge(ns.stored[i], reuse)
                        pool.tensor_tensor(res[i][:, :].rearrange("p (r c) -> p r c", c=C),
                                           cen[i][:, :].rearrange("p (r c) -> p r c", c=C),
                                           rstd[:, i, :].unsqueeze(2).to_broadcast([P, 2 * D, C]),
                                           ALU.mult).then_inc(ns.res, 1)
                def before(q):
                    return 16 * (q // 2) if q >= 2 else None
                for k in range(2 * U):
                    step(k, k % U, clear, k - lag - 2 >= 0, before(k - lag - 2))
                with pool.Fori(2, K // U) as it:
                    for u in range(U):
                        q = u - lag - 2
                        step(it * U + u, u, clear, True, it * (16 * U // 2) + 16 * (q // 2))
                for k in range(K // U * U, K + lag + 2):
                    step(k, k % U, clear and k < K, True, before(k - lag - 2))

            node_pass(n0, 0, True)
            for i in range(2):
                pool.wait_ge(n0.stored[i], 16 * ((K + 1 - i) // 2))
            for u in range(U):
                gather_group(0, u, y_rows, s_idx1, s_gather1)
            with pool.Fori(1, G // U) as it:
                for u in range(U):
                    pool.wait_ge(s_sel1, it * U + (u - U + 1))
                    gather_group(it, u, y_rows, s_idx1, s_gather1)
            node_pass(n1, 1, False)

        @block.scalar
        def _(act):
            for dst, s_ in ((dcol, dst_cols), (dprev, dst_prev_cols), (dnext, dst_next_cols)):
                act.dma_start(dst[:, :], s_).then_inc(s_edges, 16)
            act.dma_start(mb[:, :], dst_low.to_broadcast([P, T])).then_inc(s_edges, 16)
            act.dma_start(mb2[:, :], dst_rows).then_inc(s_edges, 16)
            act.dma_start(first[:, :].bitcast(I32), dst_prev_rows).then_inc(s_edges, 16)
            act.dma_start(wb[0:C, :], W1[C:2 * C, :]).then_inc(s_weights, 16)
            act.dma_start(wb[C:P, :], W1[C:2 * C, :]).then_inc(s_weights, 16)
            act.dma_start(wa[C:P, :], W1[0:C, :]).then_inc(s_weights, 16)
            act.dma_start(w2[:, :], W2).then_inc(s_weights, 16)
            act.dma_start(b1c[:, :], b1).then_inc(s_weights, 16)
            for lo in (0, C):
                act.dma_start(b2c[lo:lo + C, :], b2).then_inc(s_weights, 16)
                act.dma_start(gam[lo:lo + C, :], gamma).then_inc(s_weights, 16)
                act.dma_start(bet[lo:lo + C, :], beta).then_inc(s_weights, 16)
            act.wait_ge(s_pool, 8)
            for lo in (0, C):
                act.dma_start(bdu[lo:lo + C, lo:lo + C], U_t).then_inc(s_wu, 16)
                act.dma_start(bdv[lo:lo + C, lo:lo + C], V_t).then_inc(s_wu, 16)
            act.wait_ge(s_tab, 3)
            act.dma_start(mask_dram[0:1, :].rearrange("a (p n) -> (a p) n", p=P), carry_row[:, :]
                          ).then_inc(s_maskrows, 16)
            act.dma_start(mask_dram[1:2, :].rearrange("a (p n) -> (a p) n", p=P), reset_row[:, :]
                          ).then_inc(s_maskrows, 16)

            for c in range(XC):
                act.wait_ge(s_cen, c + 1)
                v = xs_view[:, c * XRC * C:(c + 1) * XRC * C]
                act.activation(v, v, ACT.Square).then_inc(s_sq, 1)
            act.wait_ge(s_cen, XC + 1)
            act.activation(x_tail, x_tail, ACT.Square).then_inc(s_sq, 1)
            act.wait_ge(s_st, 6)
            act.activation(cols[:, 2:3], cols[:, 1:2], ACT.Sqrt, bias=epsc[:, :]).then_inc(s_std, 1)

            def mark(g, it, u, reuse):
                act.wait_ge(s_gather[u], it * (S * 16) + S * 16)
                if reuse:
                    act.wait_ge(s_t, g - U + 1)
                for s in range(S):
                    last = act.activation(xx[u][:, s, C:2 * C], xx[u][:, s, 0:C], ACT.Copy,
                                          scale=first[:, bass.ds(g * S + s, 1)])
                last.then_inc(s_pre, 1)

            def step(g, it, u, stages, reuse):
                if 1 in stages:
                    a, ua = g - 1, (u - 1) % U
                    act.wait_ge(s_t, a + 1)
                    if reuse:
                        act.wait_ge(s_h, a - U + 2)
                    act.copy(xsxd[ua][0:C, :], ps_xt[ua % 2][0:C, :]).then_inc(s_xs, 1)
                if 2 in stages:
                    b, i = g - 2, u % 2
                    act.wait_ge(s_h, b + 1)
                    if reuse:
                        act.wait_ge(s_m, b - 1)
                    act.activation(hid[i][:, :], ps_h[i][:, :], ACT.Relu, bias=b1f[:, :]).then_inc(s_relu, 1)
                if 3 in stages:
                    d = g - 3
                    act.wait_ge(s_bt, d + 1)
                    if reuse:
                        act.wait_ge(s_sel, d)
                    act.copy(mrow[:, :, :], ps_bt[:, :, 0:C]).then_inc(s_btc, 1)
                if 0 in stages:
                    mark(g, it, u, reuse)

            act.wait_ge(s_tab, 6)
            mark(0, 0, 0, False)
            act.wait_ge(s_wready, 1)
            for g in range(1, U):
                step(g, 0, g, [q for q in range(4) if g >= q], False)
            with act.Fori(1, G // U) as it:
                for u in range(U):
                    step(it * U + u, it, u, range(4), True)
            for g in range(G, last0):
                step(g, None, g % U, [q for q in range(1, 4) if g - q < G], True)

            def node_pass(ns, lag):
                def step(k, u, ycopy, relu, square):
                    if ycopy:
                        act.wait_ge(ns.y_t, k + 1)
                        if reused(k):
                            act.wait_ge(ns.z, k - 1)
                        act.copy(y_t[u % 2][:, :], ps_h[u % 2][:, :]).then_inc(ns.y_c, 1)
                    if relu:
                        r, i = k - lag, (u - lag) % 2
                        if reused(r):
                            act.wait_ge(ns.back, r - 1)
                        if lag == 0:
                            act.activation(act_t[i][:, :], agg[:, bass.ds(r * DM, DM)], ACT.Relu,
                                           bias=b2c[:, :]).then_inc(ns.act, 1)
                        else:
                            act.wait_ge(ns.z, r + 1)
                            act.activation(act_t[i][:, :], ps_m[i][:, :], ACT.Relu).then_inc(ns.act, 1)
                    if square:
                        q, i = k - lag - 1, (u - lag - 1) % 2
                        act.wait_ge(ns.cen, q + 1)
                        if reused(q):
                            act.wait_ge(ns.ssq, q - 1)
                        act.activation(sq[i][:, :], cen[i][:, :], ACT.Square).then_inc(ns.sq, 1)
                for k in range(U):
                    step(k, k, lag == 1, k >= lag, k >= lag + 1)
                with act.Fori(1, K // U) as it:
                    for u in range(U):
                        step(it * U + u, u, lag == 1, True, True)
                for k in range(K // U * U, K + lag + 2):
                    step(k, k % U, lag == 1 and k < K, k - lag < K, k - lag - 1 < K)

            act.wait_ge(s_add, T)
            node_pass(n0, 0)
            act.wait_ge(s_add1, T)
            node_pass(n1, 1)

        @block.vector
        def _(dve):
            dve.memset(epsc[:, :], EPS).then_inc(s_const, 1)
            for t in runmax:
                dve.memset(t[C:P, :], 0.0).then_inc(s_const, 1)
            dve.wait_ge(s_pool, 8)
            dve.tensor_copy(iota_p, iota_i[:, :]).then_inc(s_const, 1)

            dve.wait_ge(s_edges, 96)
            drow, dprow = mb2, first[:, :].bitcast(I32)
            dve.tensor_tensor(carry_row[:, :], drow[:, :], dprow, ALU.is_equal).then_inc(s_tab, 1)
            dve.wait_ge(s_tab, 1)
            dve.tensor_scalar(reset_row[:, :], carry_row[:, :], 1.0, BIG, ALU.subtract, ALU.mult
                              ).then_inc(s_tab, 1)
            dve.tensor_scalar(mb[:, :], mb[:, :], 0, None, ALU.max).then_inc(s_tab, 1)
            dve.wait_ge(s_tab, 3)
            dve.tensor_scalar(mb[:, :], mb[:, :], 1, None, ALU.logical_shift_right).then_inc(s_tab, 1)
            dve.wait_ge(s_tab, 4)
            dve.tensor_scalar(mb2[:, :], mb[:, :], 1, None, ALU.logical_shift_left).then_inc(s_tab, 1)
            dve.tensor_tensor(first[:, :], dcol[:, :], dprev[:, :], ALU.not_equal).then_inc(s_tab, 1)
            dve.wait_ge(s_tab, 5)
            dve.tensor_tensor(rel[:, :], dcol[:, :], mb2[:, :], ALU.subtract).then_inc(s_tab, 1)
            dve.tensor_tensor(rel_end[:, :], dcol[:, :], dnext[:, :], ALU.is_equal).then_inc(s_tab, 1)
            dve.wait_ge(s_tab, 8)
            dve.scalar_tensor_tensor(out=rel_end[:, :], in0=rel_end[:, :], scalar=-1000.0, in1=rel[:, :],
                                     op0=ALU.mult, op1=ALU.add).then_inc(s_tab, 1)
            dve.wait_ge(s_tab, 9)

            def slots(b):
                return b[:, 0:XB * C].rearrange("p (r c) -> p c r", c=C)
            dve.wait_ge(s_sum, 1)
            dve.tensor_reduce(statrow[:, 0, 0, :], slots(ps_sum), AX.X, ALU.add).then_inc(s_st, 1)
            dve.wait_ge(s_st, 1)
            for h in range(2):
                dve.tensor_scalar(statrow[:, 0, 1 - h, :], statrow[:, 0, 0, :], 1.0 / N, None, ALU.mult
                                  ).then_inc(s_st, 1)
                dve.wait_ge(s_st, 2 + h)
            dve.tensor_copy(ps_mean, statrow[:, 0, 0, :]).then_inc(s_mean, 1)
            dve.wait_ge(s_mean, 1)
            for c in range(XC):
                v = xs_view[:, c * XRC * C:(c + 1) * XRC * C].rearrange("p (n c) -> p n c", c=C)
                dve.tensor_tensor(v, v, ps_mean.unsqueeze(1).to_broadcast([P, XRC, C]), ALU.subtract
                                  ).then_inc(s_cen, 1)
            dve.tensor_tensor(x_tail, x_tail, ps_mean[0:XT, :], ALU.subtract).then_inc(s_cen, 1)
            dve.wait_ge(s_ssq, 1)
            dve.tensor_reduce(statrow[:, 1, 0, :], slots(ps_ssq), AX.X, ALU.add).then_inc(s_st, 1)
            dve.wait_ge(s_st, 4)
            dve.tensor_scalar(statrow[:, 1, 1, :], statrow[:, 1, 0, :], 1.0, None, ALU.mult).then_inc(s_st, 1)
            dve.memset(agg[:, :], 0.0).then_inc(s_aggz, 1)
            dve.wait_ge(s_colp, 1)
            dve.tensor_scalar(cols[:, 0:1], ps_cols[:, 0:1], 1.0, None, ALU.mult)
            dve.tensor_scalar(cols[:, 1:2], ps_cols[:, 1:2], 1.0 / N, None, ALU.mult).then_inc(s_st, 1)
            dve.wait_ge(s_std, 1)
            dve.reciprocal(cols[:, 3:4], cols[:, 2:3]).then_inc(s_st, 1)
            dve.wait_ge(s_st, 7)
            dve.wait_ge(s_weights, 16 * 11)
            dve.tensor_tensor(cols[:, 4:5], cols[:, 3:4], gam[:, :], ALU.mult).then_inc(s_st, 1)
            dve.tensor_tensor(wh[C:P, :], wa[C:P, :], wb[C:P, :], ALU.subtract).then_inc(s_st, 1)
            dve.wait_ge(s_st, 9)
            dve.tensor_tensor(cols[:, 5:6], cols[:, 0:1], cols[:, 4:5], ALU.mult).then_inc(s_st, 1)
            dve.wait_ge(s_st, 10)
            dve.tensor_tensor(cols[:, 6:7], bet[:, :], cols[:, 5:6], ALU.subtract).then_inc(s_st, 1)
            dve.tensor_scalar(wh[0:C, :], wb[0:C, :], cols[0:C, 4:5], None, ALU.mult)
            dve.tensor_scalar(wh[C:P, :], wh[C:P, :], cols[C:P, 4:5], None, ALU.mult).then_inc(s_st, 1)
            dve.wait_ge(s_bias, 1)
            dve.tensor_tensor(b1f[:, :], ps_cols[:, 2:3], b1c[:, :], ALU.add).then_inc(s_st, 1)
            dve.wait_ge(s_st, 13)
            dve.wait_ge(s_aggz, 1)
            dve.memset(cols[:, 7:8], 0.0).then_inc(s_wready, 1)

            def window_starts(g):
                _, starts = nc.values_load_multi_w_load_instructions(
                    mb[0:1, bass.ds(g * S, S)], engines=[mybir.EngineType.DVE], min_val=0, max_val=N // 2 - 1,
                    skip_runtime_bounds_check_because="half of a node's number, from a table clamped at zero")
                return starts

            def add_windows(g, ps, ready, added):
                starts = window_starts(g)
                dve.wait_ge(ready, g + 1)
                for s in range(S):
                    w = agg[:, bass.ds(starts[s], MW)]
                    if s:
                        dve.wait_ge(added, g * S + s)
                    dve.tensor_tensor(w, w, ps[:, s, :], ALU.add).then_inc(added, 1)

            def build_onehot(g, i, table, ready):
                dve.tensor_tensor(onehot[i][:, :, :],
                                  iota_p.unsqueeze(1).to_broadcast([P, S, 2 * MW]),
                                  table[:, bass.ds(g * S, S)].unsqueeze(2).to_broadcast([P, S, 2 * MW]),
                                  ALU.is_equal).then_inc(ready, 1)

            def step(g, it, u, stages, reuse, first_a=False, first_b=False, first_d=False):
                if 1 in stages:
                    a, ua = g - 1, (u - 1) % U
                    ita = it if u else it - 1
                    dve.wait_ge(s_t, a + 1)
                    dve.wait_ge(s_mask[ua], ita * 32 + 32)
                    if reuse:
                        dve.wait_ge(s_h, a - U + 2)
                    if not first_a:
                        dve.wait_ge(s_xd, a)
                    dve.tensor_tensor_scan(
                        xsxd[ua][C:P, :], masks[ua][C:P, :], ps_xt[ua % 2][C:P, :],
                        0.0 if first_a else xsxd[(ua - 1) % U][C:P, GE - 1:GE], ALU.mult, ALU.add).then_inc(s_xd, 1)
                if 3 in stages:
                    d = g - 3
                    if reuse:
                        dve.wait_ge(s_sel, d)
                    build_onehot(d, 0, rel_end, s_hot)
                if 2 in stages:
                    b, i = g - 2, u % 2
                    dve.wait_ge(s_m, b + 1)
                    if reuse:
                        dve.wait_ge(s_bt, b - 1)
                    if not first_b:
                        dve.wait_ge(s_ms, b)
                    dve.tensor_tensor_scan(
                        runmax[i][0:C, :], masks[(u - 2) % U][0:C, :], ps_m[i][0:C, :],
                        0.0 if first_b else runmax[1 - i][0:C, GE - 1:GE], ALU.add, ALU.max).then_inc(s_ms, 1)
                if 3 in stages:
                    if not first_d:
                        dve.wait_ge(s_add, d * S)
                    add_windows(d, ps_sel, s_sel, s_add)

            for g in range(1, U):
                step(g, 0, g, [q for q in range(1, 4) if g >= q], False, g == 1, g == 2, g == 3)
            with dve.Fori(1, G // U) as it:
                for u in range(U):
                    step(it * U + u, it, u, range(1, 4), True)
            for g in range(G, last0):
                step(g, g // U, g % U, [q for q in range(1, 4) if g - q < G], True)

            def node_pass(ns, lag):
                def step(k, u, it, norm, squares):
                    if norm:
                        r, i = k - lag, (u - lag) % 2
                        ux = (u - lag) % U
                        itx = it if u >= lag else it - 1
                        pt = ps_xt[i][:, :]
                        rows = pt.rearrange("p (r c) -> p r c", c=C)
                        dve.wait_ge(ns.back, r + 1)
                        dve.wait_ge(ns.loaded[ux], itx * 16 + 16)
                        dve.tensor_tensor(pt, pt, xt[ux][:, :], ALU.add).then_inc(ns.v, 1)
                        dve.wait_ge(ns.v, r + 1)
                        dve.tensor_reduce(ssum[:, i, :], rows, AX.X, ALU.add).then_inc(ns.sum, 1)
                        dve.wait_ge(ns.sum, r + 1)
                        dve.tensor_scalar(nmean[:, i, :], ssum[:, i, :], 1.0 / C, None, ALU.mult).then_inc(ns.nm, 1)
                        dve.wait_ge(ns.nm, r + 1)
                        if reused(r):
                            dve.wait_ge(ns.res, r - 1)
                            dve.wait_ge(ns.sq, r - 1)
                        dve.tensor_tensor(cen[i][:, :].rearrange("p (r c) -> p r c", c=C), rows,
                                          nmean[:, i, :].unsqueeze(2).to_broadcast([P, 2 * D, C]),
                                          ALU.subtract).then_inc(ns.cen, 1)
                    if squares:
                        q, i = k - lag - 1, (u - lag - 1) % 2
                        dve.wait_ge(ns.sq, q + 1)
                        dve.tensor_reduce(ssq[:, i, :], sq[i][:, :].rearrange("p (r c) -> p r c", c=C), AX.X,
                                          ALU.add).then_inc(ns.ssq, 1)
                        dve.wait_ge(ns.ssq, q + 1)
                        if reused(q):
                            dve.wait_ge(ns.rstd, q - 1)
                        dve.tensor_scalar(var[:, i, :], ssq[:, i, :], 1.0 / C, EPS, ALU.mult, ALU.add
                                          ).then_inc(ns.var, 1)
                for k in range(U):
                    step(k, k, 0, k >= lag, k >= lag + 1)
                with dve.Fori(1, K // U) as it:
                    for u in range(U):
                        step(it * U + u, u, it, True, True)
                for k in range(K // U * U, K + lag + 1):
                    step(k, k % U, k // U, k - lag < K, k - lag - 1 < K)

            node_pass(n0, 0)

            dve.wait_ge(n0.zero, K)

            def step1(g, u, build, add, reuse, first_add=False):
                if build:
                    if reuse:
                        dve.wait_ge(s_sel1, g - 1)
                    build_onehot(g, u % 2, rel, s_hot1)
                if add:
                    if not first_add:
                        dve.wait_ge(s_add1, (g - 1) * S)
                    ps = ps_xt[(u - 1) % 2][:, 0:S * MW].rearrange("p (s m) -> p s m", s=S)
                    add_windows(g - 1, ps, s_sel1, s_add1)
            for g in range(U):
                step1(g, g, True, g >= 1, g >= 2, g == 1)
            with dve.Fori(1, G // U) as it:
                for u in range(U):
                    step1(it * U + u, u, True, True, True)
            step1(G, 0, False, True, True)
            node_pass(n1, 1)

        @block.tensor
        def _(pe):
            pe.wait_ge(s_pool, 8)

            def sum_rows(ps, ready, done):
                w = XB * C
                for c in range(XC):
                    ready(c)
                    v = xs_view[:, c * XRC * C:(c + 1) * XRC * C]
                    pe.matmul(ps[:, 0:w], ones[:, :], v[:, 0:w], start=(c == 0), stop=False)
                    with pe.Fori(1, XN) as n:
                        pe.matmul(ps[:, 0:w], ones[:, :], xs_view[:, bass.ds(n * w + c * XRC * C, w)],
                                  start=False, stop=False)
                ready(XC)
                pe.matmul(ps[:, 0:C], ones[0:XT, :], x_tail, start=False, stop=True).then_inc(done, 1)
            sum_rows(ps_sum, lambda c: pe.wait_ge(s_xl[c], 16), s_sum)
            sum_rows(ps_ssq, lambda c: pe.wait_ge(s_sq, c + 1), s_ssq)
            pe.wait_ge(s_st, 5)
            for q in range(2):
                last = pe.matmul(ps_cols[:, q:q + 1], statrow[0:1, q, :, :].rearrange("p a c -> p (a c)"),
                                 ones[0:1, 0:1], start=True, stop=True)
            last.then_inc(s_colp, 1)
            pe.wait_ge(s_st, 12)
            pe.matmul(ps_cols[:, 2:3], wa[C:P, :], cols[C:P, 6:7], start=True, stop=True).then_inc(s_bias, 1)
            pe.wait_ge(s_wready, 1)

            def step(g, u, stages, reuse, it=None):
                if 1 in stages:
                    a, ua = g - 1, (u - 1) % U
                    pe.wait_ge(s_pre, a + 1)
                    if reuse:
                        pe.wait_ge(s_xs, a - 1)
                        pe.wait_ge(s_xd, a - 1)
                    for s in range(S):
                        last = pe.transpose(ps_xt[ua % 2][:, s * P:(s + 1) * P], xx[ua][:, s, :], ident[:, :])
                    last.then_inc(s_t, 1)
                if 2 in stages:
                    b, i = g - 2, u % 2
                    pe.wait_ge(s_xs, b + 1)
                    pe.wait_ge(s_xd, b + 1)
                    if reuse:
                        pe.wait_ge(s_relu, b - 1)
                    pe.matmul(ps_h[i][:, :], wh[:, :], xsxd[(u - 2) % U][:, :], start=True, stop=True
                              ).then_inc(s_h, 1)
                if 3 in stages:
                    d, j = g - 3, (u - 3) % 2
                    pe.wait_ge(s_ms, d + 1)
                    if reuse:
                        pe.wait_ge(s_btc, d)
                    for s in range(S):
                        last = pe.transpose(ps_bt[:, s, :], runmax[j][:, s * P:(s + 1) * P], ident[:, :])
                    last.then_inc(s_bt, 1)
                if 2 in stages:
                    pe.wait_ge(s_relu, b + 1)
                    if reuse:
                        pe.wait_ge(s_ms, b - 1)
                    pe.matmul(ps_m[i][0:C, :], w2[:, :], hid[i][:, :], start=True, stop=True).then_inc(s_m, 1)
                if 3 in stages:
                    pe.wait_ge(s_btc, d + 1)
                    pe.wait_ge(s_hot, d + 1)
                    if reuse:
                        pe.wait_ge(s_add, d * S)
                    windows(lambda s: mrow[:, s, :], onehot[0], ps_sel, s_sel)

            def windows(rows, hot, ps, done):
                for s in range(S):
                    for r in range(2):
                        last = pe.matmul(ps[r * C:(r + 1) * C, s, :], rows(s), hot[:, s, r * MW:(r + 1) * MW],
                                         start=True, stop=True)
                last.then_inc(done, 1)

            for g in range(1, U):
                step(g, g, [q for q in range(1, 4) if g >= q], False)
            with pe.Fori(1, G // U) as it:
                for u in range(U):
                    step(it * U + u, u, range(1, 4), True)
            for g in range(G, last0):
                step(g, g % U, [q for q in range(1, 4) if g - q < G], True)

            def node_pass(ns, lag):
                def step(k, u, it, front, back):
                    if front:
                        pe.wait_ge(ns.loaded[u], it * 16 + 16)
                        if reused(k):
                            pe.wait_ge(ns.y_c, k - 1)
                        for j in range(D):
                            last = pe.transpose(ps_h[u % 2][:, j * P:(j + 1) * P], xt[u][:, j * P:(j + 1) * P],
                                                ident[:, :])
                        last.then_inc(ns.y_t, 1)
                    if back:
                        r, i = k - lag, (u - lag) % 2
                        if lag:
                            pe.wait_ge(ns.y_c, r + 1)
                            if reused(r):
                                pe.wait_ge(ns.act, r - 1)
                            pe.matmul(ps_m[i][:, :], bdu[:, :], y_t[i][:, :], start=True, stop=False)
                            pe.matmul(ps_m[i][:, :].rearrange("q (j p) -> q j p", j=D), bdv[:, :],
                                      agg[:, bass.ds(r * DM, DM)].rearrange("q (p j) -> q j p", j=D),
                                      start=False, stop=True).then_inc(ns.z, 1)
                        pe.wait_ge(ns.act, r + 1)
                        if reused(r):
                            pe.wait_ge(ns.cen, r - 1)
                        for j in range(D):
                            col = (act_t[i][:, :].rearrange("q (j p) -> q j p", j=D) if lag else
                                   act_t[i][:, :].rearrange("q (p j) -> q j p", j=D))[:, j, :]
                            last = pe.transpose(ps_xt[i][:, j * P:(j + 1) * P], col, ident[:, :])
                        last.then_inc(ns.back, 1)
                for k in range(U):
                    step(k, k, 0, lag == 1, k >= lag)
                with pe.Fori(1, K // U) as it:
                    for u in range(U):
                        step(it * U + u, u, it, lag == 1, True)
                for k in range(K // U * U, K + lag):
                    step(k, k % U, k // U, lag == 1 and k < K, True)

            node_pass(n0, 0)

            def step1(g, u, it, reuse):
                pe.wait_ge(s_gather1[u], it * (S * 16) + S * 16)
                pe.wait_ge(s_hot1, g + 1)
                if reuse:
                    pe.wait_ge(s_add1, (g - 1) * S)
                ps = ps_xt[u % 2][:, 0:S * MW].rearrange("p (s m) -> p s m", s=S)
                windows(lambda s: xx[u][:, s, 0:C], onehot[u % 2], ps, s_sel1)
            for g in range(U):
                step1(g, g, 0, g >= 2)
            with pe.Fori(1, G // U) as it:
                for u in range(U):
                    step1(it * U + u, u, it, True)
            pe.wait_ge(s_wu, 64)
            pe.wait_ge(s_add1, T)
            node_pass(n1, 1)


def kernel(x, src, dst, L0_gnn_gamma, L0_gnn_beta, L0_gnn_W1, L0_gnn_b1, L0_gnn_W2, L0_gnn_b2, L1_gnn_U, L1_gnn_V):
    import numpy as np
    import concourse.bacc as bacc
    from concourse.bass_utils import run_bass_kernel_spmd

    def padded(a, before, count, fill):
        full = np.concatenate([np.full((1,), fill, a.dtype), a, np.full((count + 2 - a.shape[0],), fill, a.dtype)])
        return full[1 - before:1 - before + count]

    def columns(a, tiles):
        return np.ascontiguousarray(a.reshape(tiles, P).T)

    x = np.asarray(x)
    src_r = np.asarray(src)[::-1]
    dst_r = np.asarray(dst)[::-1]
    arrays = {
        "x": np.concatenate([x, np.zeros((NP - N, C), x.dtype)]),
        "src_cols": columns(padded(src_r, 0, IDX_COLS * P, 0), IDX_COLS),
        "dst_cols": columns(padded(dst_r, 0, EP, -1), T),
        "dst_prev_cols": columns(padded(dst_r, 1, EP, -1), T),
        "dst_next_cols": columns(padded(dst_r, -1, EP, -1), T),
        "dst_rows": padded(dst_r, 0, EP, -1).reshape(P, EP // P),
        "dst_prev_rows": padded(dst_r, 1, EP, -1).reshape(P, EP // P),
        "dst_low": padded(dst_r, 0, EP, -1)[P - 1::P].reshape(1, T),
        "gamma": np.asarray(L0_gnn_gamma).reshape(C, 1),
        "beta": np.asarray(L0_gnn_beta).reshape(C, 1),
        "W1": np.asarray(L0_gnn_W1),
        "b1": np.asarray(L0_gnn_b1).reshape(HID, 1),
        "W2": np.asarray(L0_gnn_W2),
        "b2": np.asarray(L0_gnn_b2).reshape(C, 1),
        "U_t": np.asarray(L1_gnn_U).T,
        "V_t": np.asarray(L1_gnn_V).T,
    }
    nc = bacc.Bacc("TRN2", target_bir_lowering=False, num_devices=1)
    ins, args = {}, []
    for name, a in arrays.items():
        a = np.ascontiguousarray(a)
        ins[f"in_{name}"] = a
        args.append(nc.dram_tensor(f"in_{name}", a.shape, mybir.dt.from_np(a.dtype), kind="ExternalInput").ap())
    out = nc.dram_tensor("out", (NP, C), F32, kind="ExternalOutput").ap()
    gnn_kernel(nc, *args, out)
    r = run_bass_kernel_spmd(nc, [ins], core_ids=[0])
    return r.results[0]["out"][:N]
```

```python
import concourse.bass as bass
from concourse import mybir
from contextlib import ExitStack

F32 = mybir.dt.float32
BF16 = mybir.dt.bfloat16
I32 = mybir.dt.int32
ALU = mybir.AluOpType
ACT = mybir.ActivationFunctionType
AX = mybir.AxisListType

N = 50000
E = 100000
C = 64
HID = 128
P = 128
EPS = 1e-5

S = 4
GE = S * P
U = 4
G = U * -(-E // (U * GE))
T = G * S
EP = G * GE
IDX_COLS = T + U * S

MW = P // 2 + 1
D = 4
DM = D * P
K = -(-(N // 2) // DM)
MP = K * DM
NP = 2 * MP

NEED = -(-(E - N + N - (K - 1) * 2 * DM + 2 * MW) // P)
NEED_STEP = 2 * DM // P
BODY_NODES = U * GE // (2 * DM)
NODES_FROM = -(-(NEED + S) // (U * S))
BODIES = G // U
NODES_HEAD = 3
Q_IN = BODY_NODES * (BODIES - NODES_FROM)
assert BODY_NODES == 2 and NEED + NEED_STEP * (K - 1) <= T

XR = N // P
XT = N - XR * P
XC = 5
XRC = XR // XC
XB = 6
XN = XRC // XB
assert XC * XRC == XR and XB * XN == XRC

BIG = 3.0e38


def live(g):
    return not isinstance(g, int) or 0 <= g < K


def reused(g):
    return not isinstance(g, int) or g >= 2


def gnn_kernel(nc, x, src_cols, dst_cols, dst_prev_cols, dst_next_cols, dst_rows, dst_prev_rows, dst_low,
               gamma, beta, W1, b1, W2, b2, U_t, V_t, out):
    y_dram = nc.dram_tensor("y_dram", [MP, 2 * C], F32, kind="Internal").ap()
    mask_dram = nc.dram_tensor("mask_dram", [2, EP], BF16, kind="Internal").ap()

    ctx = ExitStack()
    with ctx:
        def sb(name, shape, dt=F32):
            return ctx.enter_context(nc.sbuf_tensor(name, shape, dt))

        def sem(name):
            return ctx.enter_context(nc.semaphore(name))

        agg = sb("agg", [P, MP])
        ident = sb("ident", [P, P])
        ones = sb("ones", [P, P])
        iota_i = sb("iota_i", [P, 2 * MW], I32)
        dcol = sb("dcol", [P, T], I32)
        dprev = sb("dprev", [P, T], I32)
        dnext = sb("dnext", [P, T], I32)
        mb = sb("mb", [P, T], I32)
        mb2 = sb("mb2", [P, T], I32)
        first = sb("first", [P, T])
        rel = sb("rel", [P, T])
        rel_end = sb("rel_end", [P, T])
        carry_row = sb("carry_row", [P, T], BF16)
        reset_row = sb("reset_row", [P, T], BF16)
        wb = sb("wb", [P, HID])
        wa = sb("wa", [P, HID])
        wh = sb("wh", [P, HID])
        w2 = sb("w2", [HID, C])
        b1c = sb("b1c", [P, 1])
        b1f = sb("b1f", [P, 1])
        b2c = sb("b2c", [P, 1])
        gam = sb("gam", [P, 1])
        bet = sb("bet", [P, 1])
        bdu = sb("bdu", [P, P])
        bdv = sb("bdv", [P, P])
        statrow = sb("statrow", [P, 2, 2, C])
        cols = sb("cols", [P, 8])
        epsc = sb("epsc", [P, 1])
        zero = sb("zero", [P, 1])
        idx = [sb(f"idx{h}", [P, 2 * S], I32) for h in range(2)]
        xx = [sb(f"xx{u}", [P, S, 2 * C]) for u in range(U)]
        xsxd = [sb(f"xsxd{u}", [P, GE]) for u in range(U)]
        masks = [sb(f"masks{u}", [P, GE], BF16) for u in range(U)]
        hid = [sb(f"hid{i}", [P, GE]) for i in range(2)]
        runmax = [sb(f"runmax{i}", [P, GE]) for i in range(2)]
        mrow = sb("mrow", [P, S, C])
        onehot = [sb(f"onehot{i}", [P, S, 2 * MW]) for i in range(2)]
        cmat = sb("cmat", [P, P])
        xt = [sb(f"xt{i}", [P, DM]) for i in range(2)]
        in_t = [sb(f"in_t{i}", [P, DM]) for i in range(2)]
        act_t = [sb(f"act_t{i}", [P, DM]) for i in range(2)]
        sq = sb("sq", [P, DM])
        res = [sb(f"res{i}", [P, DM]) for i in range(2)]
        ssq = sb("ssq", [P, 2, 2 * D])
        std = sb("std", [P, 2, 2 * D])
        rstd = sb("rstd", [P, 2 * D])

        bank = [ctx.enter_context(nc.psum_tensor(f"bank{i}", [P, 512], F32)) for i in range(8)]
        ps_xt, ps_h, ps_m = bank[0], bank[1], bank[2]
        ps_bt = bank[3][:, :].rearrange("p (s c) -> p s c", s=S)
        ps_sel = bank[4][:, 0:S * MW].rearrange("p (s m) -> p s m", s=S)
        iota_p = bank[4][:, 320:320 + 2 * MW]
        ps_in = bank[5]
        ps_cen = bank[6:8]
        ps_sum, ps_ssq, ps_mean, ps_cols = bank[0], bank[1], bank[2][:, 0:C], bank[3]
        ps_win = [b[:, 0:S * MW].rearrange("p (s m) -> p s m", s=S) for b in bank[0:2]]
        ps_uv = bank[2]

        s_xl = [sem(f"x_loaded{c}") for c in range(XC + 1)]
        s_edges = sem("edge_tables_loaded")
        s_weights = sem("weights_loaded")
        s_pool = sem("pool_constants")
        s_const = sem("dve_constants")
        s_wu = sem("weights_uv_loaded")
        s_tab = sem("tables_step")
        s_maskrows = sem("mask_rows_stored")
        s_sum = sem("x_summed")
        s_mean = sem("mean_ready")
        s_cen = sem("x_centred")
        s_sq = sem("x_squared")
        s_ssq = sem("squares_summed")
        s_st = sem("statistics_step")
        s_colp = sem("statistics_columns")
        s_std = sem("std_ready")
        s_bias = sem("bias_product")
        s_wready = sem("layer0_weights_ready")
        s_aggz = sem("agg_zeroed")
        s_idx = [sem(f"idx_loaded{h}") for h in range(2)]
        s_gather = [sem(f"gathered{u}") for u in range(U)]
        s_mask = [sem(f"masks_loaded{u}") for u in range(U)]
        s_clear = sem("gather_slots_clear")
        s_pre = sem("loop_rows_marked")
        s_t = sem("x_transposed")
        s_xs = sem("xs_copied")
        s_xd = sem("xd_scanned")
        s_h = sem("hidden_product")
        s_relu = sem("hidden_ready")
        s_m = sem("message_product")
        s_ms = sem("max_scanned")
        s_bt = sem("max_transposed")
        s_btc = sem("max_rows_copied")
        s_hot = sem("onehot_ready")
        s_sel = sem("windows_ready")
        s_add = sem("windows_added")
        s_idx1 = [sem(f"idx1_loaded{h}") for h in range(2)]
        s_gather1 = [sem(f"gathered1_{u}") for u in range(U)]
        s_hot1 = sem("onehot1_ready")
        s_sel1 = sem("windows1_ready")
        s_add1 = sem("windows1_added")

        class NodeSems:
            def __init__(self, tag):
                self.loaded = [sem(f"{tag}_rows_loaded{i}") for i in range(2)]
                self.t = sem(f"{tag}_rows_transposed")
                self.copy = sem(f"{tag}_rows_copied")
                self.uv = sem(f"{tag}_uv_product")
                self.act = sem(f"{tag}_relu")
                self.cen = sem(f"{tag}_centred")
                self.sq = sem(f"{tag}_squared")
                self.ssq = sem(f"{tag}_squares_summed")
                self.std = sem(f"{tag}_std")
                self.rstd = sem(f"{tag}_rstd")
                self.res = sem(f"{tag}_normed")
                self.clear = sem(f"{tag}_agg_cleared")
                self.stored = [sem(f"{tag}_stored{i}") for i in range(2)]

        class Step:
            def __init__(self, h, j):
                self.h, self.j = h, j

            def group(self, back):
                return self.h * 2 + (self.j - back)

            def slot(self, back):
                return (self.j - back) % 2

            def turns(self, back):
                return self.h + (self.j - back) // 2

        def node_steps_after(lag):
            return [Step(q // 2, q % 2) for q in range(Q_IN, K + 3 + lag)]

        n0, n1 = NodeSems("n0"), NodeSems("n1")

        x_flat = x.rearrange("(m r) c -> m (r c)", r=2)
        x_nodes = x_flat.rearrange("(k p j) c -> k p (j c)", p=P, j=D)
        y_nodes = y_dram.rearrange("(k p j) c -> k p (j c)", p=P, j=D)
        out_nodes = out.rearrange("(m r) c -> m (r c)", r=2).rearrange("(k p j) c -> k p (j c)", p=P, j=D)
        y_rows = y_dram.rearrange("m (r c) -> (m r) c", r=2)
        x_stat = x[0:XR * P, :].rearrange("(p n) c -> p (n c)", p=P)
        xs_view = agg[:, 0:XR * C]
        x_tail = agg[0:XT, XR * C:XR * C + C]

        last0, last1 = G + 3, G + 1

        block = ctx.enter_context(nc.Block())

        @block.sync
        def _(sp):
            for h in range(2):
                sp.dma_start(idx[h][:, :], src_cols[:, 2 * S * h:2 * S * (h + 1)]).then_inc(s_idx[h], 16)
            for c in range(XC):
                sp.dma_start(xs_view[:, c * XRC * C:(c + 1) * XRC * C],
                             x_stat[:, c * XRC * C:(c + 1) * XRC * C]).then_inc(s_xl[c], 16)
            sp.dma_start(x_tail, x[XR * P:N, :]).then_inc(s_xl[XC], 16)
            sp.wait_ge(s_maskrows, 32)

            def load_masks(g, u, reuse):
                if reuse:
                    sp.wait_ge(s_ms, g - U + 1)
                for row, lo in ((1, 0), (0, C)):
                    sp.dma_start(masks[u][lo:lo + C, :],
                                 mask_dram[row:row + 1, bass.ds(g * GE, GE)].to_broadcast([C, GE])
                                 ).then_inc(s_mask[u], 16)

            def load_idx(it, h, gathered, loaded):
                for u in (2 * h, 2 * h + 1):
                    sp.wait_ge(gathered[u], it * S * 16 + S * 16)
                sp.dma_start(idx[h][:, :],
                             src_cols[:, bass.ds(it * (U * S) + (U * S + 2 * S * h), 2 * S)]).then_inc(loaded[h], 16)

            def body0(it, reuse):
                for h in range(2):
                    for u in (2 * h, 2 * h + 1):
                        load_masks(it * U + u, u, reuse)
                    load_idx(it, h, s_gather, s_idx)

            def node_step(q, ns, src, dst, lag):
                if live(q.group(-1)):
                    if reused(q.group(-1)):
                        sp.wait_ge(ns.t, q.group(0))
                    node_load(q.group(-1), q.slot(-1), ns, src)
                if live(q.group(lag + 3)):
                    sp.wait_ge(ns.res, q.group(lag + 2))
                    sp.dma_start(dst[bass.ds(q.group(lag + 3) * -1 + (K - 1), 1), :, :].rearrange("k p c -> (k p) c"),
                                 res[q.slot(lag + 3)][:, :]).then_inc(ns.stored[q.slot(lag + 3)], 16)

            def node_load(g, i, ns, src):
                sp.dma_start(xt[i][:, :], src[bass.ds(g * -1 + (K - 1), 1), :, :].rearrange("k p c -> (k p) c")
                             ).then_inc(ns.loaded[i], 16)

            def all_stored(ns):
                for i in range(2):
                    sp.wait_ge(ns.stored[i], 16 * ((K + 1 - i) // 2))

            def nodes0(h, j):
                node_step(Step(h, j), n0, x_nodes, y_nodes, 0)

            def nodes1(h, j):
                node_step(Step(h, j), n1, y_nodes, out_nodes, 1)

            def no_nodes(h, j):
                pass

            def body0(it, reuse, nodes):
                for h in range(2):
                    for u in (2 * h, 2 * h + 1):
                        load_masks(it * U + u, u, reuse)
                    load_idx(it, h, s_gather, s_idx)
                    nodes(it - NODES_FROM, h)

            body0(0, False, no_nodes)
            with sp.Fori(1, NODES_FROM) as it:
                body0(it, True, no_nodes)
            node_load(0, 0, n0, x_nodes)
            for it in range(NODES_FROM, NODES_FROM + NODES_HEAD):
                body0(it, True, nodes0)
            with sp.Fori(NODES_FROM + NODES_HEAD, BODIES) as it:
                body0(it, True, nodes0)
            for q in node_steps_after(0):
                node_step(q, n0, x_nodes, y_nodes, 0)
            all_stored(n0)

            for h in range(2):
                sp.dma_start(idx[h][:, :], src_cols[:, 2 * S * h:2 * S * (h + 1)]).then_inc(s_idx1[h], 16)
            node_load(0, 0, n1, y_nodes)

            def body1(it, nodes):
                for h in range(2):
                    load_idx(it, h, s_gather1, s_idx1)
                    nodes(it - NODES_FROM, h)

            body1(0, no_nodes)
            with sp.Fori(1, NODES_FROM) as it:
                body1(it, no_nodes)
            for it in range(NODES_FROM, NODES_FROM + NODES_HEAD):
                body1(it, nodes1)
            with sp.Fori(NODES_FROM + NODES_HEAD, BODIES) as it:
                body1(it, nodes1)
            for q in node_steps_after(1):
                node_step(q, n1, y_nodes, out_nodes, 1)
            all_stored(n1)
            for h in range(2):
                sp.wait_ge(s_idx[h], 16 * (BODIES + 1))
                sp.wait_ge(s_idx1[h], 16 * (BODIES + 1))

        @block.gpsimd
        def _(pool):
            pool.memset(ident[:, :], 0.0).then_inc(s_pool, 1)
            pool.memset(ones[:, :], 1.0).then_inc(s_pool, 1)
            pool.memset(zero[:, :], 0.0).then_inc(s_pool, 1)
            pool.memset(bdu[:, :], 0.0).then_inc(s_pool, 1)
            pool.memset(bdv[:, :], 0.0).then_inc(s_pool, 1)
            pool.iota(iota_i[:, :], pattern=[[1, 2], [2, MW]], base=0, channel_multiplier=0).then_inc(s_pool, 1)
            pool.wait_ge(s_pool, 6)
            pool.affine_select(out=ident[:, :], in_=ident[:, :], compare_op=ALU.not_equal, fill=1.0,
                               base=0, pattern=[[-1, P]], channel_multiplier=1).then_inc(s_pool, 1)

            def gather_group(it, u, table, loaded, gathered):
                h = u // 2
                if u % 2 == 0:
                    pool.wait_ge(loaded[h], it * 16 + 16)
                pool.sem_inc(s_clear, 1)
                for s in range(S):
                    col = (u % 2) * S + s
                    pool.indirect_dma_start(out=xx[u][:, s, 0:C], out_offset=None, in_=table,
                                            in_offset=bass.IndirectOffsetOnAxis(ap=idx[h][:, col:col + 1], axis=0),
                                            ).then_inc(gathered[u], 16)

            for u in range(U):
                gather_group(0, u, x, s_idx, s_gather)
            with pool.Fori(1, G // U) as it:
                for u in range(U):
                    pool.wait_ge(s_t, it * U + (u - U + 1))
                    gather_group(it, u, x, s_idx, s_gather)

            for i in range(2):
                pool.wait_ge(n0.stored[i], 16 * ((K + 1 - i) // 2))
            for u in range(U):
                gather_group(0, u, y_rows, s_idx1, s_gather1)
            with pool.Fori(1, G // U) as it:
                for u in range(U):
                    pool.wait_ge(s_sel1, it * U + (u - U + 1))
                    gather_group(it, u, y_rows, s_idx1, s_gather1)

        @block.scalar
        def _(act):
            for dst, s_ in ((dcol, dst_cols), (dprev, dst_prev_cols), (dnext, dst_next_cols)):
                act.dma_start(dst[:, :], s_).then_inc(s_edges, 16)
            act.dma_start(mb[:, :], dst_low.to_broadcast([P, T])).then_inc(s_edges, 16)
            act.dma_start(mb2[:, :], dst_rows).then_inc(s_edges, 16)
            act.dma_start(first[:, :].bitcast(I32), dst_prev_rows).then_inc(s_edges, 16)
            act.dma_start(wb[0:C, :], W1[C:2 * C, :]).then_inc(s_weights, 16)
            act.dma_start(wb[C:P, :], W1[C:2 * C, :]).then_inc(s_weights, 16)
            act.dma_start(wa[C:P, :], W1[0:C, :]).then_inc(s_weights, 16)
            act.dma_start(w2[:, :], W2).then_inc(s_weights, 16)
            act.dma_start(b1c[:, :], b1).then_inc(s_weights, 16)
            for lo in (0, C):
                act.dma_start(b2c[lo:lo + C, :], b2).then_inc(s_weights, 16)
                act.dma_start(gam[lo:lo + C, :], gamma).then_inc(s_weights, 16)
                act.dma_start(bet[lo:lo + C, :], beta).then_inc(s_weights, 16)
            act.wait_ge(s_pool, 7)
            for lo in (0, C):
                act.dma_start(bdu[lo:lo + C, lo:lo + C], U_t).then_inc(s_wu, 16)
                act.dma_start(bdv[lo:lo + C, lo:lo + C], V_t).then_inc(s_wu, 16)
            act.wait_ge(s_tab, 3)
            act.dma_start(mask_dram[0:1, :].rearrange("a (p n) -> (a p) n", p=P), carry_row[:, :]
                          ).then_inc(s_maskrows, 16)
            act.dma_start(mask_dram[1:2, :].rearrange("a (p n) -> (a p) n", p=P), reset_row[:, :]
                          ).then_inc(s_maskrows, 16)

            for c in range(XC):
                act.wait_ge(s_cen, c + 1)
                v = xs_view[:, c * XRC * C:(c + 1) * XRC * C]
                act.activation(v, v, ACT.Square).then_inc(s_sq, 1)
            act.wait_ge(s_cen, XC + 1)
            act.activation(x_tail, x_tail, ACT.Square).then_inc(s_sq, 1)
            act.wait_ge(s_st, 6)
            act.activation(cols[:, 2:3], cols[:, 1:2], ACT.Sqrt, bias=epsc[:, :]).then_inc(s_std, 1)

            def mark(g, it, u, reuse):
                act.wait_ge(s_gather[u], it * (S * 16) + S * 16)
                if reuse:
                    act.wait_ge(s_t, g - U + 1)
                for s in range(S):
                    last = act.activation(xx[u][:, s, C:2 * C], xx[u][:, s, 0:C], ACT.Copy,
                                          scale=first[:, bass.ds(g * S + s, 1)])
                last.then_inc(s_pre, 1)

            def step(g, it, u, stages, reuse):
                if 1 in stages:
                    a, ua = g - 1, (u - 1) % U
                    act.wait_ge(s_t, a + 1)
                    if reuse:
                        act.wait_ge(s_h, a - U + 2)
                    act.copy(xsxd[ua][0:C, :], ps_xt[0:C, :]).then_inc(s_xs, 1)
                if 2 in stages:
                    b, i = g - 2, u % 2
                    act.wait_ge(s_h, b + 1)
                    if reuse:
                        act.wait_ge(s_m, b - 1)
                    act.activation(hid[i][:, :], ps_h[:, :], ACT.Relu, bias=b1f[:, :]).then_inc(s_relu, 1)
                if 3 in stages:
                    d = g - 3
                    act.wait_ge(s_bt, d + 1)
                    if reuse:
                        act.wait_ge(s_sel, d)
                    act.copy(mrow[:, :, :], ps_bt[:, :, 0:C]).then_inc(s_btc, 1)
                if 0 in stages:
                    mark(g, it, u, reuse)

            act.wait_ge(s_tab, 6)
            mark(0, 0, 0, False)
            act.wait_ge(s_wready, 1)
            for g in range(1, U):
                step(g, 0, g, [q for q in range(4) if g >= q], False)

            def node_step(q, ns, lag):
                back = lag + 1
                if live(q.group(back + 1)):
                    act.wait_ge(ns.ssq, q.group(back))
                    i = q.slot(back + 1)
                    if reused(q.group(back + 1)):
                        act.wait_ge(ns.rstd, q.group(back + 2))
                    act.activation(std[:, i, :], ssq[:, i, :], ACT.Sqrt, bias=epsc[:, :], scale=1.0 / C
                                   ).then_inc(ns.std, 1)
                if live(q.group(lag)):
                    r, i = q.group(lag), q.slot(lag)
                    if reused(r):
                        act.wait_ge(ns.cen, q.group(lag + 1))
                    if lag:
                        act.wait_ge(ns.uv, q.group(lag - 1))
                        act.activation(act_t[i][:, :], ps_uv[:, :], ACT.Relu).then_inc(ns.act, 1)
                    else:
                        act.wait_ge(s_add, r * NEED_STEP + NEED)
                        act.activation(act_t[i][:, :], agg[:, bass.ds(r * -DM + (K - 1) * DM, DM)], ACT.Relu,
                                       bias=b2c[:, :]).then_inc(ns.act, 1)
                if live(q.group(0)):
                    act.wait_ge(ns.t, q.group(-1))
                    if reused(q.group(0)):
                        act.wait_ge(ns.cen, q.group(1))
                    act.copy(in_t[q.slot(0)][:, :], ps_in[:, :]).then_inc(ns.copy, 1)
                if live(q.group(back)):
                    act.wait_ge(ns.cen, q.group(back - 1))
                    if not isinstance(q.h, int) or q.group(back) >= 1:
                        act.wait_ge(ns.ssq, q.group(back))
                    act.activation(sq[:, :], ps_cen[q.slot(back)][:, :], ACT.Square).then_inc(ns.sq, 1)

            def body0(it, nodes):
                for u in range(U):
                    step(it * U + u, it, u, range(4), True)
                    if u % 2:
                        nodes(it - NODES_FROM, u // 2)

            def nodes0(h, j):
                node_step(Step(h, j), n0, 0)

            def nodes1(h, j):
                node_step(Step(h, j), n1, 1)

            with act.Fori(1, NODES_FROM) as it:
                body0(it, lambda h, j: None)
            for it in range(NODES_FROM, NODES_FROM + NODES_HEAD):
                body0(it, nodes0)
            with act.Fori(NODES_FROM + NODES_HEAD, BODIES) as it:
                body0(it, nodes0)
            for g in range(G, last0):
                step(g, None, g % U, [q for q in range(1, 4) if g - q < G], True)
            for q in node_steps_after(0):
                node_step(q, n0, 0)

            for it in range(NODES_FROM, NODES_FROM + NODES_HEAD):
                for j in range(2):
                    nodes1(it - NODES_FROM, j)
            with act.Fori(NODES_FROM + NODES_HEAD, BODIES) as it:
                for j in range(2):
                    nodes1(it - NODES_FROM, j)
            for q in node_steps_after(1):
                node_step(q, n1, 1)

        @block.vector
        def _(dve):
            dve.memset(epsc[:, :], EPS).then_inc(s_const, 1)
            for t in runmax:
                dve.memset(t[C:P, :], 0.0).then_inc(s_const, 1)
            dve.wait_ge(s_pool, 7)
            dve.tensor_copy(iota_p, iota_i[:, :]).then_inc(s_const, 1)
            dve.memset(cmat[:, :], 0.0).then_inc(s_const, 1)
            dve.wait_ge(s_const, 5)
            for lo in (0, C):
                dve.memset(cmat[lo:lo + C, lo:lo + C], -1.0 / C).then_inc(s_const, 1)
            dve.wait_ge(s_const, 7)
            dve.tensor_tensor(cmat[:, :], cmat[:, :], ident[:, :], ALU.add).then_inc(s_const, 1)

            dve.wait_ge(s_edges, 96)
            drow, dprow = mb2, first[:, :].bitcast(I32)
            dve.tensor_tensor(carry_row[:, :], drow[:, :], dprow, ALU.is_equal).then_inc(s_tab, 1)
            dve.wait_ge(s_tab, 1)
            dve.tensor_scalar(reset_row[:, :], carry_row[:, :], 1.0, BIG, ALU.subtract, ALU.mult
                              ).then_inc(s_tab, 1)
            dve.tensor_scalar(mb[:, :], mb[:, :], 0, None, ALU.max).then_inc(s_tab, 1)
            dve.wait_ge(s_tab, 3)
            dve.tensor_scalar(mb[:, :], mb[:, :], 1, None, ALU.logical_shift_right).then_inc(s_tab, 1)
            dve.wait_ge(s_tab, 4)
            dve.tensor_scalar(mb2[:, :], mb[:, :], 1, None, ALU.logical_shift_left).then_inc(s_tab, 1)
            dve.tensor_tensor(first[:, :], dcol[:, :], dprev[:, :], ALU.not_equal).then_inc(s_tab, 1)
            dve.wait_ge(s_tab, 5)
            dve.tensor_tensor(rel[:, :], dcol[:, :], mb2[:, :], ALU.subtract).then_inc(s_tab, 1)
            dve.tensor_tensor(rel_end[:, :], dcol[:, :], dnext[:, :], ALU.is_equal).then_inc(s_tab, 1)
            dve.wait_ge(s_tab, 8)
            dve.scalar_tensor_tensor(out=rel_end[:, :], in0=rel_end[:, :], scalar=-1000.0, in1=rel[:, :],
                                     op0=ALU.mult, op1=ALU.add).then_inc(s_tab, 1)
            dve.wait_ge(s_tab, 9)

            def slots(b):
                return b[:, 0:XB * C].rearrange("p (r c) -> p c r", c=C)
            dve.wait_ge(s_sum, 1)
            dve.tensor_reduce(statrow[:, 0, 0, :], slots(ps_sum), AX.X, ALU.add).then_inc(s_st, 1)
            dve.wait_ge(s_st, 1)
            for h in range(2):
                dve.tensor_scalar(statrow[:, 0, 1 - h, :], statrow[:, 0, 0, :], 1.0 / N, None, ALU.mult
                                  ).then_inc(s_st, 1)
                dve.wait_ge(s_st, 2 + h)
            dve.tensor_copy(ps_mean, statrow[:, 0, 0, :]).then_inc(s_mean, 1)
            dve.wait_ge(s_mean, 1)
            for c in range(XC):
                v = xs_view[:, c * XRC * C:(c + 1) * XRC * C].rearrange("p (n c) -> p n c", c=C)
                dve.tensor_tensor(v, v, ps_mean.unsqueeze(1).to_broadcast([P, XRC, C]), ALU.subtract
                                  ).then_inc(s_cen, 1)
            dve.tensor_tensor(x_tail, x_tail, ps_mean[0:XT, :], ALU.subtract).then_inc(s_cen, 1)
            dve.wait_ge(s_ssq, 1)
            dve.tensor_reduce(statrow[:, 1, 0, :], slots(ps_ssq), AX.X, ALU.add).then_inc(s_st, 1)
            dve.wait_ge(s_st, 4)
            dve.tensor_scalar(statrow[:, 1, 1, :], statrow[:, 1, 0, :], 1.0, None, ALU.mult).then_inc(s_st, 1)
            dve.memset(agg[:, :], 0.0).then_inc(s_aggz, 1)
            dve.wait_ge(s_colp, 1)
            dve.tensor_scalar(cols[:, 0:1], ps_cols[:, 0:1], 1.0, None, ALU.mult)
            dve.tensor_scalar(cols[:, 1:2], ps_cols[:, 1:2], 1.0 / N, None, ALU.mult).then_inc(s_st, 1)
            dve.wait_ge(s_std, 1)
            dve.reciprocal(cols[:, 3:4], cols[:, 2:3]).then_inc(s_st, 1)
            dve.wait_ge(s_st, 7)
            dve.wait_ge(s_weights, 16 * 11)
            dve.tensor_tensor(cols[:, 4:5], cols[:, 3:4], gam[:, :], ALU.mult).then_inc(s_st, 1)
            dve.tensor_tensor(wh[C:P, :], wa[C:P, :], wb[C:P, :], ALU.subtract).then_inc(s_st, 1)
            dve.wait_ge(s_st, 9)
            dve.tensor_tensor(cols[:, 5:6], cols[:, 0:1], cols[:, 4:5], ALU.mult).then_inc(s_st, 1)
            dve.wait_ge(s_st, 10)
            dve.tensor_tensor(cols[:, 6:7], bet[:, :], cols[:, 5:6], ALU.subtract).then_inc(s_st, 1)
            dve.tensor_scalar(wh[0:C, :], wb[0:C, :], cols[0:C, 4:5], None, ALU.mult)
            dve.tensor_scalar(wh[C:P, :], wh[C:P, :], cols[C:P, 4:5], None, ALU.mult).then_inc(s_st, 1)
            dve.wait_ge(s_bias, 1)
            dve.tensor_tensor(b1f[:, :], ps_cols[:, 2:3], b1c[:, :], ALU.add).then_inc(s_st, 1)
            dve.wait_ge(s_st, 13)
            dve.wait_ge(s_aggz, 1)
            dve.memset(cols[:, 7:8], 0.0).then_inc(s_wready, 1)

            def window_starts(g):
                _, starts = nc.values_load_multi_w_load_instructions(
                    mb[0:1, bass.ds(g * S, S)], engines=[mybir.EngineType.DVE], min_val=0, max_val=N // 2 - 1,
                    skip_runtime_bounds_check_because="half of a node's number, from a table clamped at zero")
                return starts

            def add_windows(g, ps, ready, added):
                starts = window_starts(g)
                dve.wait_ge(ready, g + 1)
                for s in range(S):
                    w = agg[:, bass.ds(starts[s], MW)]
                    if s:
                        dve.wait_ge(added, g * S + s)
                    dve.tensor_tensor(w, w, ps[:, s, :], ALU.add).then_inc(added, 1)

            def build_onehot(g, i, table, ready):
                dve.tensor_tensor(onehot[i][:, :, :],
                                  iota_p.unsqueeze(1).to_broadcast([P, S, 2 * MW]),
                                  table[:, bass.ds(g * S, S)].unsqueeze(2).to_broadcast([P, S, 2 * MW]),
                                  ALU.is_equal).then_inc(ready, 1)

            def step(g, it, u, stages, reuse, first_a=False, first_b=False, first_d=False):
                if 1 in stages:
                    a, ua = g - 1, (u - 1) % U
                    ita = it if u else it - 1
                    dve.wait_ge(s_t, a + 1)
                    dve.wait_ge(s_mask[ua], ita * 32 + 32)
                    if reuse:
                        dve.wait_ge(s_h, a - U + 2)
                    if not first_a:
                        dve.wait_ge(s_xd, a)
                    dve.tensor_tensor_scan(
                        xsxd[ua][C:P, :], masks[ua][C:P, :], ps_xt[C:P, :],
                        0.0 if first_a else xsxd[(ua - 1) % U][C:P, GE - 1:GE], ALU.mult, ALU.add).then_inc(s_xd, 1)
                if 3 in stages:
                    d = g - 3
                    if reuse:
                        dve.wait_ge(s_sel, d)
                    build_onehot(d, 0, rel_end, s_hot)
                if 2 in stages:
                    b, i = g - 2, u % 2
                    dve.wait_ge(s_m, b + 1)
                    if reuse:
                        dve.wait_ge(s_bt, b - 1)
                    if not first_b:
                        dve.wait_ge(s_ms, b)
                    dve.tensor_tensor_scan(
                        runmax[i][0:C, :], masks[(u - 2) % U][0:C, :], ps_m[0:C, :],
                        0.0 if first_b else runmax[1 - i][0:C, GE - 1:GE], ALU.add, ALU.max).then_inc(s_ms, 1)
                if 3 in stages:
                    if not first_d:
                        dve.wait_ge(s_add, d * S)
                    add_windows(d, ps_sel, s_sel, s_add)

            for g in range(1, U):
                step(g, 0, g, [q for q in range(1, 4) if g >= q], False, g == 1, g == 2, g == 3)

            def node_step(q, ns, lag, clear):
                back = lag + 1
                if live(q.group(back + 1)):
                    i = q.slot(back + 1)
                    dve.wait_ge(ns.std, q.group(back))
                    if not isinstance(q.h, int) or q.group(back + 1) >= 1:
                        dve.wait_ge(ns.res, q.group(back + 1))
                    dve.reciprocal(rstd[:, :], std[:, i, :]).then_inc(ns.rstd, 1)
                    dve.wait_ge(ns.rstd, q.group(back))
                    if reused(q.group(back + 1)):
                        dve.wait_ge(ns.stored[i], q.turns(back + 1) * 16)
                    dve.tensor_tensor(res[i][:, :].rearrange("p (r c) -> p r c", c=C),
                                      ps_cen[i][:, :].rearrange("p (r c) -> p r c", c=C),
                                      rstd[:, :].unsqueeze(2).to_broadcast([P, 2 * D, C]), ALU.mult
                                      ).then_inc(ns.res, 1)
                if live(q.group(back)):
                    i = q.slot(back)
                    dve.wait_ge(ns.sq, q.group(back - 1))
                    if reused(q.group(back)):
                        dve.wait_ge(ns.std, q.group(back + 1))
                    dve.tensor_reduce(ssq[:, i, :], sq[:, :].rearrange("p (r c) -> p r c", c=C), AX.X, ALU.add
                                      ).then_inc(ns.ssq, 1)
                if clear and live(q.group(1)):
                    dve.wait_ge(ns.act, q.group(0))
                    dve.tensor_copy(agg[:, bass.ds(q.group(1) * -DM + (K - 1) * DM, DM)],
                                    zero[:, :].to_broadcast([P, DM])).then_inc(ns.clear, 1)

            def nodes0(h, j):
                node_step(Step(h, j), n0, 0, True)

            def nodes1(h, j):
                node_step(Step(h, j), n1, 1, False)

            def no_nodes(h, j):
                pass

            def body0(it, nodes):
                for u in range(U):
                    step(it * U + u, it, u, range(1, 4), True)
                    if u % 2:
                        nodes(it - NODES_FROM, u // 2)

            with dve.Fori(1, NODES_FROM) as it:
                body0(it, no_nodes)
            for it in range(NODES_FROM, NODES_FROM + NODES_HEAD):
                body0(it, nodes0)
            with dve.Fori(NODES_FROM + NODES_HEAD, BODIES) as it:
                body0(it, nodes0)
            for g in range(G, last0):
                step(g, g // U, g % U, [q for q in range(1, 4) if g - q < G], True)
            for q in node_steps_after(0):
                node_step(q, n0, 0, True)

            dve.wait_ge(n0.clear, K)

            def step1(g, u, build, add, reuse, first_add=False):
                if build:
                    if reuse:
                        dve.wait_ge(s_sel1, g - 1)
                    build_onehot(g, u % 2, rel, s_hot1)
                if add:
                    if not first_add:
                        dve.wait_ge(s_add1, (g - 1) * S)
                    add_windows(g - 1, ps_win[(u - 1) % 2], s_sel1, s_add1)

            def body1(it, nodes):
                for u in range(U):
                    step1(it * U + u, u, True, True, True)
                    if u % 2:
                        nodes(it - NODES_FROM, u // 2)

            for g in range(U):
                step1(g, g, True, g >= 1, g >= 2, g == 1)
            with dve.Fori(1, NODES_FROM) as it:
                body1(it, no_nodes)
            for it in range(NODES_FROM, NODES_FROM + NODES_HEAD):
                body1(it, nodes1)
            with dve.Fori(NODES_FROM + NODES_HEAD, BODIES) as it:
                body1(it, nodes1)
            step1(G, 0, False, True, True)
            for q in node_steps_after(1):
                node_step(q, n1, 1, False)

        @block.tensor
        def _(pe):
            pe.wait_ge(s_pool, 7)

            def sum_rows(ps, ready, done):
                w = XB * C
                for c in range(XC):
                    ready(c)
                    v = xs_view[:, c * XRC * C:(c + 1) * XRC * C]
                    pe.matmul(ps[:, 0:w], ones[:, :], v[:, 0:w], start=(c == 0), stop=False)
                    with pe.Fori(1, XN) as n:
                        pe.matmul(ps[:, 0:w], ones[:, :], xs_view[:, bass.ds(n * w + c * XRC * C, w)],
                                  start=False, stop=False)
                ready(XC)
                pe.matmul(ps[:, 0:C], ones[0:XT, :], x_tail, start=False, stop=True).then_inc(done, 1)
            sum_rows(ps_sum, lambda c: pe.wait_ge(s_xl[c], 16), s_sum)
            sum_rows(ps_ssq, lambda c: pe.wait_ge(s_sq, c + 1), s_ssq)
            pe.wait_ge(s_st, 5)
            for q in range(2):
                last = pe.matmul(ps_cols[:, q:q + 1], statrow[0:1, q, :, :].rearrange("p a c -> p (a c)"),
                                 ones[0:1, 0:1], start=True, stop=True)
            last.then_inc(s_colp, 1)
            pe.wait_ge(s_st, 12)
            pe.matmul(ps_cols[:, 2:3], wa[C:P, :], cols[C:P, 6:7], start=True, stop=True).then_inc(s_bias, 1)
            pe.wait_ge(s_wready, 1)
            pe.wait_ge(s_const, 8)

            def step(g, u, stages, reuse, it=None):
                if 1 in stages:
                    a, ua = g - 1, (u - 1) % U
                    pe.wait_ge(s_pre, a + 1)
                    if reuse:
                        pe.wait_ge(s_xs, a)
                        pe.wait_ge(s_xd, a)
                    for s in range(S):
                        last = pe.transpose(ps_xt[:, s * P:(s + 1) * P], xx[ua][:, s, :], ident[:, :])
                    last.then_inc(s_t, 1)
                if 2 in stages:
                    b, i = g - 2, u % 2
                    pe.wait_ge(s_xs, b + 1)
                    pe.wait_ge(s_xd, b + 1)
                    if reuse:
                        pe.wait_ge(s_relu, b)
                    pe.matmul(ps_h[:, :], wh[:, :], xsxd[(u - 2) % U][:, :], start=True, stop=True
                              ).then_inc(s_h, 1)
                if 3 in stages:
                    d, j = g - 3, (u - 3) % 2
                    pe.wait_ge(s_ms, d + 1)
                    if reuse:
                        pe.wait_ge(s_btc, d)
                    for s in range(S):
                        last = pe.transpose(ps_bt[:, s, :], runmax[j][:, s * P:(s + 1) * P], ident[:, :])
                    last.then_inc(s_bt, 1)
                if 2 in stages:
                    pe.wait_ge(s_relu, b + 1)
                    if reuse:
                        pe.wait_ge(s_ms, b)
                    pe.matmul(ps_m[0:C, :], w2[:, :], hid[i][:, :], start=True, stop=True).then_inc(s_m, 1)
                if 3 in stages:
                    pe.wait_ge(s_btc, d + 1)
                    pe.wait_ge(s_hot, d + 1)
                    if reuse:
                        pe.wait_ge(s_add, d * S)
                    windows(lambda s: mrow[:, s, :], onehot[0], ps_sel, s_sel)

            def windows(rows, hot, ps, done):
                for s in range(S):
                    for r in range(2):
                        last = pe.matmul(ps[r * C:(r + 1) * C, s, :], rows(s), hot[:, s, r * MW:(r + 1) * MW],
                                         start=True, stop=True)
                last.then_inc(done, 1)

            def node_step(q, ns, lag):
                if live(q.group(lag + 1)):
                    e, i = q.group(lag + 1), q.slot(lag + 1)
                    pe.wait_ge(ns.copy, q.group(lag))
                    pe.wait_ge(ns.act, q.group(lag))
                    if reused(e):
                        pe.wait_ge(ns.res, q.group(lag + 2))
                    for j in range(D):
                        a = (act_t[i][:, :].rearrange("q (j p) -> q j p", j=D) if lag else
                             act_t[i][:, :].rearrange("q (p j) -> q j p", j=D))[:, j, :]
                        dst = ps_cen[i][:, j * P:(j + 1) * P]
                        pe.matmul(dst, a, cmat[:, :], start=True, stop=False)
                        last = pe.matmul(dst, in_t[i][:, j * P:(j + 1) * P], cmat[:, :], start=False, stop=True)
                    last.then_inc(ns.cen, 1)
                if lag and live(q.group(1)):
                    r, i = q.group(1), q.slot(1)
                    pe.wait_ge(ns.copy, q.group(0))
                    pe.wait_ge(s_add1, r * NEED_STEP + NEED)
                    if not isinstance(r, int) or r >= 1:
                        pe.wait_ge(ns.act, r)
                    pe.matmul(ps_uv[:, :], bdu[:, :], in_t[i][:, :], start=True, stop=False)
                    pe.matmul(ps_uv[:, :].rearrange("q (j p) -> q j p", j=D), bdv[:, :],
                              agg[:, bass.ds(r * -DM + (K - 1) * DM, DM)].rearrange("q (p j) -> q j p", j=D),
                              start=False, stop=True).then_inc(ns.uv, 1)
                if live(q.group(0)):
                    i = q.slot(0)
                    pe.wait_ge(ns.loaded[i], q.turns(0) * 16 + 16)
                    if not isinstance(q.h, int) or q.group(0) >= 1:
                        pe.wait_ge(ns.copy, q.group(0))
                    for j in range(D):
                        last = pe.transpose(ps_in[:, j * P:(j + 1) * P], xt[i][:, j * P:(j + 1) * P], ident[:, :])
                    last.then_inc(ns.t, 1)

            def nodes0(h, j):
                node_step(Step(h, j), n0, 0)

            def nodes1(h, j):
                node_step(Step(h, j), n1, 1)

            def no_nodes(h, j):
                pass

            def body0(it, nodes):
                for u in range(U):
                    step(it * U + u, u, range(1, 4), True)
                    if u % 2 == 0:
                        nodes(it - NODES_FROM, u // 2)

            for g in range(1, U):
                step(g, g, [q for q in range(1, 4) if g >= q], g >= 2)
            with pe.Fori(1, NODES_FROM) as it:
                body0(it, no_nodes)
            for it in range(NODES_FROM, NODES_FROM + NODES_HEAD):
                body0(it, nodes0)
            with pe.Fori(NODES_FROM + NODES_HEAD, BODIES) as it:
                body0(it, nodes0)
            for g in range(G, last0):
                step(g, g % U, [q for q in range(1, 4) if g - q < G], True)
            for q in node_steps_after(0):
                node_step(q, n0, 0)

            def step1(g, u, it, reuse):
                pe.wait_ge(s_gather1[u], it * (S * 16) + S * 16)
                pe.wait_ge(s_hot1, g + 1)
                if reuse:
                    pe.wait_ge(s_add1, (g - 1) * S)
                windows(lambda s: xx[u][:, s, 0:C], onehot[u % 2], ps_win[u % 2], s_sel1)

            def body1(it, nodes):
                for u in range(U):
                    step1(it * U + u, u, it, True)
                    if u % 2 == 0:
                        nodes(it - NODES_FROM, u // 2)

            for g in range(U):
                step1(g, g, 0, g >= 2)
            with pe.Fori(1, NODES_FROM) as it:
                body1(it, no_nodes)
            pe.wait_ge(s_wu, 64)
            for it in range(NODES_FROM, NODES_FROM + NODES_HEAD):
                body1(it, nodes1)
            with pe.Fori(NODES_FROM + NODES_HEAD, BODIES) as it:
                body1(it, nodes1)
            for q in node_steps_after(1):
                node_step(q, n1, 1)


def kernel(x, src, dst, L0_gnn_gamma, L0_gnn_beta, L0_gnn_W1, L0_gnn_b1, L0_gnn_W2, L0_gnn_b2, L1_gnn_U, L1_gnn_V):
    import numpy as np
    import concourse.bacc as bacc
    from concourse.bass_utils import run_bass_kernel_spmd

    def padded(a, before, count, fill):
        full = np.concatenate([np.full((1,), fill, a.dtype), a, np.full((count + 2 - a.shape[0],), fill, a.dtype)])
        return full[1 - before:1 - before + count]

    def columns(a, tiles):
        return np.ascontiguousarray(a.reshape(tiles, P).T)

    x = np.asarray(x)
    src_r = np.asarray(src)[::-1]
    dst_r = np.asarray(dst)[::-1]
    arrays = {
        "x": np.concatenate([x, np.zeros((NP - N, C), x.dtype)]),
        "src_cols": columns(padded(src_r, 0, IDX_COLS * P, 0), IDX_COLS),
        "dst_cols": columns(padded(dst_r, 0, EP, -1), T),
        "dst_prev_cols": columns(padded(dst_r, 1, EP, -1), T),
        "dst_next_cols": columns(padded(dst_r, -1, EP, -1), T),
        "dst_rows": padded(dst_r, 0, EP, -1).reshape(P, EP // P),
        "dst_prev_rows": padded(dst_r, 1, EP, -1).reshape(P, EP // P),
        "dst_low": padded(dst_r, 0, EP, -1)[P - 1::P].reshape(1, T),
        "gamma": np.asarray(L0_gnn_gamma).reshape(C, 1),
        "beta": np.asarray(L0_gnn_beta).reshape(C, 1),
        "W1": np.asarray(L0_gnn_W1),
        "b1": np.asarray(L0_gnn_b1).reshape(HID, 1),
        "W2": np.asarray(L0_gnn_W2),
        "b2": np.asarray(L0_gnn_b2).reshape(C, 1),
        "U_t": np.asarray(L1_gnn_U).T,
        "V_t": np.asarray(L1_gnn_V).T,
    }
    nc = bacc.Bacc("TRN2", target_bir_lowering=False, num_devices=1)
    ins, args = {}, []
    for name, a in arrays.items():
        a = np.ascontiguousarray(a)
        ins[f"in_{name}"] = a
        args.append(nc.dram_tensor(f"in_{name}", a.shape, mybir.dt.from_np(a.dtype), kind="ExternalInput").ap())
    out = nc.dram_tensor("out", (NP, C), F32, kind="ExternalOutput").ap()
    gnn_kernel(nc, *args, out)
    r = run_bass_kernel_spmd(nc, [ins], core_ids=[0])
    return r.results[0]["out"][:N]
```

```python
import concourse.bass as bass
from concourse import mybir
from contextlib import ExitStack

F32 = mybir.dt.float32
BF16 = mybir.dt.bfloat16
I32 = mybir.dt.int32
ALU = mybir.AluOpType
ACT = mybir.ActivationFunctionType
AX = mybir.AxisListType

N = 50000
E = 100000
C = 64
HID = 128
P = 128
EPS = 1e-5

S = 4
GE = S * P
U = 4
G = U * -(-E // (U * GE))
T = G * S
EP = G * GE
IDX_COLS = T + U * S

MW = P // 2 + 1
D = 4
DM = D * P
K = -(-(N // 2) // DM)
MP = K * DM
NP = 2 * MP

NEED_STEP = 2 * DM // P
NEED = max(-(-(E - N + N - (K - 1) * 2 * DM + 2 * MW) // P), T - NEED_STEP * (K - 1))
BODY_NODES = U * GE // (2 * DM)
NODES_FROM = -(-(NEED + S) // (U * S))
DEPTH = 6
HEAD = 2
BODIES = G // U
NODES_HEAD = 3
Q_IN = BODY_NODES * (BODIES - NODES_FROM)
NODES1_FROM = NODES_FROM - 2
NODES1_HEAD = 4
Q1_IN = BODY_NODES * (BODIES - NODES1_FROM) - 1
Q_DRAINED = Q_IN + DEPTH // 2
assert DEPTH % 2 == 0 and BODY_NODES == 2 and NEED + NEED_STEP * (K - 1) <= T

SC = 512
CHUNKS = -(-(N // 2) // SC)
LOADS = (8, 8, 8, 8, 8, 5, CHUNKS - 45)
assert LOADS[-1] > 0


BIG = 3.0e38


def past(n):
    return not isinstance(n, int) or n > 0


def live(g):
    return not isinstance(g, int) or 0 <= g < K


def reused(g):
    return not isinstance(g, int) or g >= 2


def gnn_kernel(nc, x, x_pairs, src_cols, dst_cols, dst_prev_cols, dst_next_cols, dst_rows, dst_prev_rows, dst_low,
               gamma, beta, W1, b1, W2, b2, U_t, V_t, out):
    y_dram = nc.dram_tensor("y_dram", [MP, 2 * C], F32, kind="Internal").ap()
    mask_dram = nc.dram_tensor("mask_dram", [2, EP], BF16, kind="Internal").ap()

    ctx = ExitStack()
    with ctx:
        def sb(name, shape, dt=F32):
            return ctx.enter_context(nc.sbuf_tensor(name, shape, dt))

        def sem(name):
            return ctx.enter_context(nc.semaphore(name))

        agg = sb("agg", [P, MP])
        ident = sb("ident", [P, P])
        iota_i = sb("iota_i", [P, 2 * MW], I32)
        dcol = sb("dcol", [P, T], I32)
        dprev = sb("dprev", [P, T], I32)
        dnext = sb("dnext", [P, T], I32)
        mb = sb("mb", [P, T], I32)
        mb2 = sb("mb2", [P, T], I32)
        first = sb("first", [P, T])
        rel = sb("rel", [P, T])
        rel_end = sb("rel_end", [P, T])
        carry_row = sb("carry_row", [P, T], BF16)
        reset_row = sb("reset_row", [P, T], BF16)
        wb = sb("wb", [P, HID])
        wa = sb("wa", [P, HID])
        wh = sb("wh", [P, HID])
        w2 = sb("w2", [HID, C])
        b1c = sb("b1c", [P, 1])
        b1f = sb("b1f", [P, 1])
        b2c = sb("b2c", [P, 1])
        gam = sb("gam", [P, 1])
        bet = sb("bet", [P, 1])
        bdu = sb("bdu", [P, P])
        bdv = sb("bdv", [P, P])
        halves = sb("halves", [P, P])
        bn = sb("bn", [P, CHUNKS, 6])
        mv = sb("mv", [P, 2])
        cols = sb("cols", [P, 10])
        epsc = sb("epsc", [P, 1])
        zero = sb("zero", [P, 1])
        idx = [sb(f"idx{h}", [P, 2 * S], I32) for h in range(2)]
        xx = [sb(f"xx{u}", [P, S, 2 * C]) for u in range(U)]
        xsxd = [sb(f"xsxd{u}", [P, GE]) for u in range(U)]
        masks = [sb(f"masks{u}", [P, GE], BF16) for u in range(U)]
        hid = [sb(f"hid{i}", [P, GE]) for i in range(2)]
        runmax = [sb(f"runmax{i}", [C, GE]) for i in range(2)]
        mrow = [sb(f"mrow{i}", [P, S, C]) for i in range(2)]
        onehot = [sb(f"onehot{i}", [P, S, 2 * MW]) for i in range(2)]
        cmat = sb("cmat", [P, P])
        xt = [sb(f"xt{i}", [P, DM]) for i in range(2)]
        in_t = [sb(f"in_t{i}", [P, DM]) for i in range(2)]
        act_t = sb("act_t", [P, DM])
        res_t = sb("res_t", [P, DM])
        sq = sb("sq", [P, DM])
        res = [sb(f"res{i}", [P, DM]) for i in range(2)]
        ssq = sb("ssq", [P, 2, 2 * D])
        std = sb("std", [P, 2, 2 * D])
        rstd = sb("rstd", [P, 2 * D])

        bank = [ctx.enter_context(nc.psum_tensor(f"bank{i}", [P, 512], F32)) for i in range(8)]
        ps_xt, ps_h, ps_m = bank[0], bank[1], bank[2]
        ps_bt = ps_m[:, 0:S * C].rearrange("p (s c) -> p s c", s=S)
        ps_sel = [b[:, 0:S * MW].rearrange("p (s m) -> p s m", s=S) for b in bank[3:5]]
        iota_p = bank[4][:, 320:320 + 2 * MW]
        ps_in = bank[5]
        ps_cen = bank[6:8]
        ps_cols = bank[3]
        ps_win = [b[:, 0:S * MW].rearrange("p (s m) -> p s m", s=S) for b in bank[0:2]]
        ps_uv = bank[2]

        s_xl = [sem(f"x_loaded{c}") for c in range(len(LOADS))]
        s_edges = sem("edge_tables_loaded")
        s_weights = sem("weights_loaded")
        s_pool = sem("pool_constants")
        s_const = sem("dve_constants")
        s_wu = sem("weights_uv_loaded")
        s_tab = sem("tables_step")
        s_maskrows = sem("mask_rows_stored")
        s_bn = sem("load_statistics")
        s_st = sem("statistics_step")
        s_colp = sem("statistics_columns")
        s_std = sem("std_ready")
        s_bias = sem("bias_product")
        s_wready = sem("layer0_weights_ready")
        s_aggz = sem("agg_zeroed")
        s_idx = [sem(f"idx_loaded{h}") for h in range(2)]
        s_gather = [sem(f"gathered{u}") for u in range(U)]
        s_carry = [sem(f"carry_masks_loaded{u}") for u in range(U)]
        s_reset = [sem(f"reset_masks_loaded{u}") for u in range(U)]
        s_clear = sem("gather_slots_clear")
        s_pre = sem("loop_rows_marked")
        s_t = sem("x_transposed")
        s_xs = sem("xs_copied")
        s_xd = sem("xd_scanned")
        s_h = sem("hidden_product")
        s_relu = sem("hidden_ready")
        s_m = sem("message_product")
        s_ms = sem("max_scanned")
        s_bt = sem("max_transposed")
        s_btc = sem("max_rows_copied")
        s_hot = sem("onehot_ready")
        s_sel = sem("windows_ready")
        s_add = sem("windows_added")
        s_idx1 = [sem(f"idx1_loaded{h}") for h in range(2)]
        s_gather1 = [sem(f"gathered1_{u}") for u in range(U)]
        s_hot1 = sem("onehot1_ready")
        s_sel1 = sem("windows1_ready")
        s_add1 = sem("windows1_added")

        class NodeSems:
            def __init__(self, tag):
                self.loaded = [sem(f"{tag}_rows_loaded{i}") for i in range(2)]
                self.t = sem(f"{tag}_rows_transposed")
                self.copy = sem(f"{tag}_rows_copied")
                self.uv = sem(f"{tag}_uv_product")
                self.act = sem(f"{tag}_relu")
                self.sum = sem(f"{tag}_residual")
                self.cen = sem(f"{tag}_centred")
                self.sq = sem(f"{tag}_squared")
                self.ssq = sem(f"{tag}_squares_summed")
                self.std = sem(f"{tag}_std")
                self.rstd = sem(f"{tag}_rstd")
                self.res = sem(f"{tag}_normed")
                self.clear = sem(f"{tag}_agg_cleared")
                self.stored = [sem(f"{tag}_stored{i}") for i in range(2)]

        class Step:
            def __init__(self, h, j):
                self.h, self.j = h, j

            def group(self, back):
                return self.h * 2 + (self.j - back)

            def slot(self, back):
                return (self.j - back) % 2

            def turns(self, back):
                return self.h + (self.j - back) // 2

        def node_steps(q0, lag):
            return [Step(q // 2, q % 2) for q in range(q0, K + 3 + lag)]

        n0, n1 = NodeSems("n0"), NodeSems("n1")

        y_nodes = y_dram.rearrange("(k p j) c -> k p (j c)", p=P, j=D)
        out_nodes = out.rearrange("(m r) c -> m (r c)", r=2).rearrange("(k p j) c -> k p (j c)", p=P, j=D)
        y_rows = y_dram.rearrange("m (r c) -> (m r) c", r=2)

        def stages(g):
            return [q for q in range(DEPTH + 1) if 0 <= g - q < G]

        block = ctx.enter_context(nc.Block())

        @block.sync
        def _(sp):
            for h in range(2):
                sp.dma_start(idx[h][:, :], src_cols[:, 2 * S * h:2 * S * (h + 1)]).then_inc(s_idx[h], 16)
            for dst, s_ in ((mb2, dst_rows), (first[:, :].bitcast(I32), dst_prev_rows), (dcol, dst_cols)):
                sp.dma_start(dst[:, :], s_).then_inc(s_edges, 16)
            for c, n in enumerate(LOADS):
                lo = sum(LOADS[:c]) * SC
                hi = min(lo + n * SC, N // 2)
                sp.dma_start(agg[:, lo:hi], x_pairs[:, lo:hi]).then_inc(s_xl[c], 16)

            def load_idx(it, h, gathered, loaded):
                for u in (2 * h, 2 * h + 1):
                    sp.wait_ge(gathered[u], it * S * 16 + S * 16)
                sp.dma_start(idx[h][:, :],
                             src_cols[:, bass.ds(it * (U * S) + (U * S + 2 * S * h), 2 * S)]).then_inc(loaded[h], 16)

            for h in range(2):
                load_idx(0, h, s_gather, s_idx)
            sp.wait_ge(s_maskrows, 32)

            def load_masks(g, u, reuse):
                for row, lo, loaded, scanned in ((0, C, s_carry, s_xd), (1, 0, s_reset, s_ms)):
                    if reuse:
                        sp.wait_ge(scanned, g - U + 1)
                    sp.dma_start(masks[u][lo:lo + C, :],
                                 mask_dram[row:row + 1, bass.ds(g * GE, GE)].to_broadcast([C, GE])
                                 ).then_inc(loaded[u], 16)

            def node_step(q, ns, dst, lag):
                if live(q.group(-1)):
                    if reused(q.group(-1)):
                        sp.wait_ge(ns.t if lag else ns.sum, q.group(0))
                    node_load(q.group(-1), q.slot(-1), ns, lag)
                if live(q.group(lag + 3)):
                    sp.wait_ge(ns.res, q.group(lag + 2))
                    sp.dma_start(dst[bass.ds(q.group(lag + 3) * -1 + (K - 1), 1), :, :].rearrange("k p c -> (k p) c"),
                                 res[q.slot(lag + 3)][:, :]).then_inc(ns.stored[q.slot(lag + 3)], 16)

            def node_load(g, i, ns, lag):
                if lag:
                    sp.dma_start(xt[i][:, :], y_nodes[bass.ds(g * -1 + (K - 1), 1), :, :].rearrange("k p c -> (k p) c")
                                 ).then_inc(ns.loaded[i], 16)
                else:
                    sp.dma_start(xt[i][:, :], x_pairs[:, bass.ds(g * -DM + (K - 1) * DM, DM)]
                                 ).then_inc(ns.loaded[i], 16)

            def all_stored(ns):
                for i in range(2):
                    sp.wait_ge(ns.stored[i], 16 * ((K + 1 - i) // 2))

            def nodes0(h, j):
                node_step(Step(h, j), n0, y_nodes, 0)

            def nodes1(h, j):
                node_step(Step(h, j), n1, out_nodes, 1)

            def no_nodes(h, j):
                pass

            def body0(it, reuse, nodes):
                for h in range(2):
                    for u in (2 * h, 2 * h + 1):
                        load_masks(it * U + u, u, reuse)
                    if reuse:
                        load_idx(it, h, s_gather, s_idx)
                    nodes(it - NODES_FROM, h)

            body0(0, False, no_nodes)
            with sp.Fori(1, NODES_FROM) as it:
                body0(it, True, no_nodes)
            node_load(0, 0, n0, 0)
            for it in range(NODES_FROM, NODES_FROM + NODES_HEAD):
                body0(it, True, nodes0)
            with sp.Fori(NODES_FROM + NODES_HEAD, BODIES) as it:
                body0(it, True, nodes0)
            for q in node_steps(Q_IN, 0):
                node_step(q, n0, y_nodes, 0)
            all_stored(n0)

            for h in range(2):
                sp.dma_start(idx[h][:, :], src_cols[:, 2 * S * h:2 * S * (h + 1)]).then_inc(s_idx1[h], 16)

            def body1(it, nodes):
                for h in range(2):
                    load_idx(it, h, s_gather1, s_idx1)
                    nodes(it - NODES1_FROM, h - 1)

            body1(0, no_nodes)
            with sp.Fori(1, NODES1_FROM) as it:
                body1(it, no_nodes)
            for it in range(NODES1_FROM, NODES1_FROM + NODES1_HEAD):
                body1(it, nodes1)
            with sp.Fori(NODES1_FROM + NODES1_HEAD, BODIES - 1) as it:
                body1(it, nodes1)
            body1(BODIES - 1, nodes1)
            for q in node_steps(Q1_IN, 1):
                node_step(q, n1, out_nodes, 1)
            all_stored(n1)
            for h in range(2):
                sp.wait_ge(s_idx[h], 16 * (BODIES + 1))
                sp.wait_ge(s_idx1[h], 16 * (BODIES + 1))

        @block.gpsimd
        def _(pool):
            pool.memset(ident[:, :], 0.0).then_inc(s_pool, 1)
            pool.memset(zero[:, :], 0.0).then_inc(s_pool, 1)
            pool.memset(bdu[:, :], 0.0).then_inc(s_pool, 1)
            pool.memset(bdv[:, :], 0.0).then_inc(s_pool, 1)
            pool.iota(iota_i[:, :], pattern=[[1, 2], [2, MW]], base=0, channel_multiplier=0).then_inc(s_pool, 1)
            pool.wait_ge(s_pool, 5)
            pool.affine_select(out=ident[:, :], in_=ident[:, :], compare_op=ALU.not_equal, fill=1.0,
                               base=0, pattern=[[-1, P]], channel_multiplier=1).then_inc(s_pool, 1)

            def gather_group(it, u, table, loaded, gathered):
                h = u // 2
                if u % 2 == 0:
                    pool.wait_ge(loaded[h], it * 16 + 16)
                pool.sem_inc(s_clear, 1)
                for s in range(S):
                    col = (u % 2) * S + s
                    pool.indirect_dma_start(out=xx[u][:, s, 0:C], out_offset=None, in_=table,
                                            in_offset=bass.IndirectOffsetOnAxis(ap=idx[h][:, col:col + 1], axis=0),
                                            ).then_inc(gathered[u], 16)

            for u in range(U):
                gather_group(0, u, x, s_idx, s_gather)
            pool.memset(agg[:, N // 2:MP], 0.0).then_inc(s_aggz, 1)
            for c, n in enumerate(LOADS):
                lo = sum(LOADS[:c])
                pool.wait_ge(s_bn, lo + n)
                pool.memset(agg[:, lo * SC:min((lo + n) * SC, N // 2)], 0.0).then_inc(s_aggz, 1)
            with pool.Fori(1, G // U) as it:
                for u in range(U):
                    pool.wait_ge(s_t, it * U + (u - U + 1))
                    gather_group(it, u, x, s_idx, s_gather)

            for i in range(2):
                pool.wait_ge(n0.stored[i], 16 * ((K + 1 - i) // 2))
            for u in range(U):
                gather_group(0, u, y_rows, s_idx1, s_gather1)
            with pool.Fori(1, G // U) as it:
                for u in range(U):
                    pool.wait_ge(s_sel1, it * U + (u - U + 1))
                    gather_group(it, u, y_rows, s_idx1, s_gather1)

        @block.scalar
        def _(act):
            for dst, s_ in ((dprev, dst_prev_cols), (dnext, dst_next_cols)):
                act.dma_start(dst[:, :], s_).then_inc(s_edges, 16)
            act.dma_start(mb[:, :], dst_low.to_broadcast([P, T])).then_inc(s_edges, 16)
            act.dma_start(wb[0:C, :], W1[C:2 * C, :]).then_inc(s_weights, 16)
            act.dma_start(wb[C:P, :], W1[C:2 * C, :]).then_inc(s_weights, 16)
            act.dma_start(wa[C:P, :], W1[0:C, :]).then_inc(s_weights, 16)
            act.dma_start(w2[:, :], W2).then_inc(s_weights, 16)
            act.dma_start(b1c[:, :], b1).then_inc(s_weights, 16)
            for lo in (0, C):
                act.dma_start(b2c[lo:lo + C, :], b2).then_inc(s_weights, 16)
                act.dma_start(gam[lo:lo + C, :], gamma).then_inc(s_weights, 16)
                act.dma_start(bet[lo:lo + C, :], beta).then_inc(s_weights, 16)
            act.wait_ge(s_pool, 6)
            for lo in (0, C):
                act.dma_start(bdu[lo:lo + C, lo:lo + C], U_t).then_inc(s_wu, 16)
                act.dma_start(bdv[lo:lo + C, lo:lo + C], V_t).then_inc(s_wu, 16)
            act.wait_ge(s_tab, 3)
            act.dma_start(mask_dram[0:1, :].rearrange("a (p n) -> (a p) n", p=P), carry_row[:, :]
                          ).then_inc(s_maskrows, 16)
            act.dma_start(mask_dram[1:2, :].rearrange("a (p n) -> (a p) n", p=P), reset_row[:, :]
                          ).then_inc(s_maskrows, 16)

            def mark(g, it, u):
                act.wait_ge(s_gather[u], it * (S * 16) + S * 16)
                if past(g - U + 1):
                    act.wait_ge(s_t, g - U + 1)
                for s in range(S):
                    last = act.activation(xx[u][:, s, C:2 * C], xx[u][:, s, 0:C], ACT.Copy,
                                          scale=first[:, bass.ds(g * S + s, 1)])
                last.then_inc(s_pre, 1)

            def step(g, it, u, has):
                if 1 in has:
                    a, ua = g - 1, (u - 1) % U
                    act.wait_ge(s_t, a + 1)
                    if past(a - U + 2):
                        act.wait_ge(s_h, a - U + 2)
                    act.copy(xsxd[ua][0:C, :], ps_xt[0:C, :]).then_inc(s_xs, 1)
                if 4 in has:
                    d = g - 4
                    act.wait_ge(s_bt, d + 1)
                    if past(d - 1):
                        act.wait_ge(s_sel, d - 1)
                    act.copy(mrow[u % 2][:, :, :], ps_bt).then_inc(s_btc, 1)
                if 0 in has:
                    mark(g, it, u)
                if 2 in has:
                    b, i = g - 2, u % 2
                    act.wait_ge(s_h, b + 1)
                    if past(b - 1):
                        act.wait_ge(s_m, b - 1)
                    act.activation(hid[i][:, :], ps_h[:, :], ACT.Relu, bias=b1f[:, :]).then_inc(s_relu, 1)

            act.wait_ge(s_tab, 6)
            mark(0, 0, 0)
            step(1, 0, 1, [0, 1])
            act.wait_ge(s_colp, 2)
            act.activation(cols[:, 2:3], ps_cols[:, 1:2], ACT.Sqrt, bias=epsc[:, :]).then_inc(s_std, 1)

            step(2, 0, 2, [0, 1])
            act.wait_ge(s_wready, 1)
            step(2, 0, 2, [2])
            for g in range(3, HEAD * U):
                step(g, g // U, g % U, stages(g))

            def node_relu(q, ns, lag):
                if not lag and live(q.group(0)):
                    r = q.group(0)
                    if past(r):
                        act.wait_ge(ns.sum, r)
                    act.wait_ge(s_add, r * NEED_STEP + NEED)
                    act.activation(act_t[:, :], agg[:, bass.ds(r * -DM + (K - 1) * DM, DM)], ACT.Relu,
                                   bias=b2c[:, :]).then_inc(ns.act, 1)
                if not lag and live(q.group(1)):
                    if isinstance(q.group(1), int):
                        act.wait_ge(ns.act, q.group(0))
                    act.copy(agg[:, bass.ds(q.group(1) * -DM + (K - 1) * DM, DM)],
                             zero[:, :].to_broadcast([P, DM])).then_inc(ns.clear, 1)
                if lag and live(q.group(0)):
                    act.wait_ge(ns.t, q.group(-1))
                    if past(q.group(1)):
                        act.wait_ge(ns.sum, q.group(1))
                    act.copy(in_t[q.slot(0)][:, :], ps_in[:, :]).then_inc(ns.copy, 1)

            def node_root(q, ns, lag):
                back = lag + 1
                if live(q.group(back + 1)):
                    act.wait_ge(ns.ssq, q.group(back))
                    i = q.slot(back + 1)
                    if past(q.group(back + 2)):
                        act.wait_ge(ns.rstd, q.group(back + 2))
                    act.activation(std[:, i, :], ssq[:, i, :], ACT.Sqrt, bias=epsc[:, :], scale=1.0 / C
                                   ).then_inc(ns.std, 1)
                if live(q.group(back)):
                    act.wait_ge(ns.cen, q.group(back - 1))
                    if past(q.group(back)):
                        act.wait_ge(ns.ssq, q.group(back))
                    act.activation(sq[:, :], ps_cen[q.slot(back)][:, :], ACT.Square).then_inc(ns.sq, 1)

            def part0(g, it, u, has, nodes=True):
                step(g, it, u, has)
                if nodes and u % 2 == 0:
                    node_root(Step(it - NODES_FROM, u // 2 - 1), n0, 0)
                if nodes and u % 2:
                    node_relu(Step(it - NODES_FROM, u // 2), n0, 0)

            def body0(it, nodes=True):
                for u in range(U):
                    part0(it * U + u, it, u, range(DEPTH + 1), nodes)

            with act.Fori(HEAD, NODES_FROM) as it:
                body0(it, False)
            for it in range(NODES_FROM, NODES_FROM + NODES_HEAD):
                body0(it)
            with act.Fori(NODES_FROM + NODES_HEAD, BODIES) as it:
                body0(it)
            for g in range(G, G + DEPTH):
                part0(g, g // U, g % U, stages(g))
            node_root(Step(0, Q_DRAINED - 1), n0, 0)
            for q in node_steps(Q_DRAINED, 0):
                node_relu(q, n0, 0)
                node_root(q, n0, 0)

            def nodes1(q):
                node_relu(q, n1, 1)
                node_root(q, n1, 1)

            for it in range(NODES1_FROM, NODES1_FROM + NODES1_HEAD):
                for j in range(2):
                    nodes1(Step(it - NODES1_FROM, j - 1))
            with act.Fori(NODES1_FROM + NODES1_HEAD, BODIES) as it:
                for j in range(2):
                    nodes1(Step(it - NODES1_FROM, j - 1))
            for q in node_steps(Q1_IN, 1):
                nodes1(q)

        @block.vector
        def _(dve):
            dve.memset(epsc[:, :], EPS).then_inc(s_const, 1)
            dve.wait_ge(s_pool, 6)
            dve.tensor_copy(iota_p, iota_i[:, :]).then_inc(s_const, 1)
            dve.memset(cmat[:, :], 0.0).then_inc(s_const, 1)
            dve.wait_ge(s_const, 3)
            for lo in (0, C):
                dve.memset(cmat[lo:lo + C, lo:lo + C], -1.0 / C).then_inc(s_const, 1)
            dve.wait_ge(s_const, 5)
            dve.tensor_tensor(cmat[:, :], cmat[:, :], ident[:, :], ALU.add).then_inc(s_const, 1)
            for lo in (0, C):
                for to in (0, C):
                    dve.tensor_scalar(halves[lo:lo + C, to:to + C], ident[lo:lo + C, lo:lo + C], 0.5, None, ALU.mult
                                      ).then_inc(s_const, 1)

            def window_starts(g):
                _, starts = nc.values_load_multi_w_load_instructions(
                    mb[0:1, bass.ds(g * S, S)], engines=[mybir.EngineType.DVE], min_val=0, max_val=N // 2 - 1,
                    skip_runtime_bounds_check_because="half of a node's number, from a table clamped at zero")
                return starts

            def add_window(g, s, starts, ps, added):
                w = agg[:, bass.ds(starts[s], MW)]
                if past(g * S + s):
                    dve.wait_ge(added, g * S + s)
                dve.tensor_tensor(w, w, ps[:, s, :], ALU.add).then_inc(added, 1)

            def build_onehot(g, i, table, ready):
                dve.tensor_tensor(onehot[i][:, :, :],
                                  iota_p.unsqueeze(1).to_broadcast([P, S, 2 * MW]),
                                  table[:, bass.ds(g * S, S)].unsqueeze(2).to_broadcast([P, S, 2 * MW]),
                                  ALU.is_equal).then_inc(ready, 1)

            def step(g, it, u, has, between=lambda: None):
                f = g - 6
                if 6 in has:
                    starts = window_starts(f)
                    if isinstance(f, int) and f == 0:
                        dve.wait_ge(s_aggz, len(LOADS) + 1)
                    dve.wait_ge(s_sel, f + 1)
                    add_window(f, 0, starts, ps_sel[u % 2], s_add)
                if 1 in has:
                    a, ua = g - 1, (u - 1) % U
                    dve.wait_ge(s_t, a + 1)
                    dve.wait_ge(s_carry[ua], (it if u >= 1 else it - 1) * 16 + 16)
                    if past(a - U + 2):
                        dve.wait_ge(s_h, a - U + 2)
                    start = 0.0
                    if past(a):
                        dve.wait_ge(s_xd, a)
                        start = xsxd[(ua - 1) % U][C:P, GE - 1:GE]
                    dve.tensor_tensor_scan(xsxd[ua][C:P, :], masks[ua][C:P, :], ps_xt[C:P, :], start,
                                           ALU.mult, ALU.add).then_inc(s_xd, 1)
                if 6 in has:
                    add_window(f, 1, starts, ps_sel[u % 2], s_add)
                if 5 in has:
                    e = g - 5
                    if past(e - 1):
                        dve.wait_ge(s_sel, e - 1)
                    build_onehot(e, (u - 5) % 2, rel_end, s_hot)
                if 6 in has:
                    add_window(f, 2, starts, ps_sel[u % 2], s_add)
                between()
                if 6 in has:
                    for s in range(3, S):
                        add_window(f, s, starts, ps_sel[u % 2], s_add)
                if 3 in has:
                    c, i, uc = g - 3, (u - 3) % 2, (u - 3) % U
                    dve.wait_ge(s_m, c + 1)
                    dve.wait_ge(s_reset[uc], (it if u >= 3 else it - 1) * 16 + 16)
                    if past(c - 1):
                        dve.wait_ge(s_bt, c - 1)
                    start = 0.0
                    if past(c):
                        dve.wait_ge(s_ms, c)
                        start = runmax[1 - i][0:C, GE - 1:GE]
                    dve.tensor_tensor_scan(runmax[i][0:C, :], masks[uc][0:C, :], ps_m[0:C, :], start,
                                           ALU.add, ALU.max).then_inc(s_ms, 1)

            dve.wait_ge(s_edges, 96)
            drow, dprow = mb2, first[:, :].bitcast(I32)
            dve.tensor_tensor(carry_row[:, :], drow[:, :], dprow, ALU.is_equal).then_inc(s_tab, 1)
            dve.wait_ge(s_tab, 1)
            dve.tensor_scalar(reset_row[:, :], carry_row[:, :], 1.0, BIG, ALU.subtract, ALU.mult
                              ).then_inc(s_tab, 1)
            dve.tensor_scalar(mb[:, :], mb[:, :], 0, None, ALU.max).then_inc(s_tab, 1)
            dve.wait_ge(s_tab, 3)
            dve.tensor_scalar(mb[:, :], mb[:, :], 1, None, ALU.logical_shift_right).then_inc(s_tab, 1)
            dve.wait_ge(s_tab, 4)
            dve.tensor_scalar(mb2[:, :], mb[:, :], 1, None, ALU.logical_shift_left).then_inc(s_tab, 1)
            dve.tensor_tensor(first[:, :], dcol[:, :], dprev[:, :], ALU.not_equal).then_inc(s_tab, 1)
            dve.wait_ge(s_tab, 5)
            dve.tensor_tensor(rel[:, :], dcol[:, :], mb2[:, :], ALU.subtract).then_inc(s_tab, 1)
            dve.tensor_tensor(rel_end[:, :], dcol[:, :], dnext[:, :], ALU.is_equal).then_inc(s_tab, 1)
            dve.wait_ge(s_tab, 8)
            dve.scalar_tensor_tensor(out=rel_end[:, :], in0=rel_end[:, :], scalar=-1000.0, in1=rel[:, :],
                                     op0=ALU.mult, op1=ALU.add).then_inc(s_tab, 1)
            dve.wait_ge(s_tab, 9)

            for c, n in enumerate(LOADS):
                dve.wait_ge(s_xl[c], 16)
                for k in range(sum(LOADS[:c]), sum(LOADS[:c + 1])):
                    dve.bn_stats(bn[:, k, :], agg[:, k * SC:min((k + 1) * SC, N // 2)]).then_inc(s_bn, 1)
            dve.wait_ge(s_bn, CHUNKS)
            dve.bn_aggr(mv[:, :], bn[:, :, :].rearrange("p k q -> p (k q)")).then_inc(s_st, 1)
            dve.wait_ge(s_colp, 1)
            dve.tensor_scalar(cols[:, 0:1], ps_cols[:, 0:1], 1.0, None, ALU.mult).then_inc(s_st, 1)
            dve.wait_ge(s_st, 2)
            dve.tensor_tensor(cols[:, 7:8], mv[:, 0:1], cols[:, 0:1], ALU.subtract).then_inc(s_st, 1)
            dve.wait_ge(s_st, 3)
            dve.tensor_tensor(cols[:, 8:9], cols[:, 7:8], cols[:, 7:8], ALU.mult).then_inc(s_st, 1)
            dve.wait_ge(s_st, 4)
            dve.tensor_tensor(cols[:, 1:2], cols[:, 8:9], mv[:, 1:2], ALU.add).then_inc(s_st, 1)
            dve.wait_ge(s_weights, 16 * 11)
            dve.tensor_tensor(wh[C:P, :], wa[C:P, :], wb[C:P, :], ALU.subtract).then_inc(s_st, 1)
            step(1, 0, 1, [1])
            dve.wait_ge(s_std, 1)
            dve.reciprocal(cols[:, 3:4], cols[:, 2:3]).then_inc(s_st, 1)
            dve.wait_ge(s_st, 7)
            dve.tensor_tensor(cols[:, 4:5], cols[:, 3:4], gam[:, :], ALU.mult).then_inc(s_st, 1)
            dve.wait_ge(s_st, 8)
            dve.tensor_tensor(cols[:, 5:6], cols[:, 0:1], cols[:, 4:5], ALU.mult).then_inc(s_st, 1)
            dve.wait_ge(s_st, 9)
            dve.tensor_tensor(cols[:, 6:7], bet[:, :], cols[:, 5:6], ALU.subtract).then_inc(s_st, 1)
            dve.tensor_scalar(wh[0:C, :], wb[0:C, :], cols[0:C, 4:5], None, ALU.mult)
            dve.tensor_scalar(wh[C:P, :], wh[C:P, :], cols[C:P, 4:5], None, ALU.mult).then_inc(s_st, 1)
            dve.wait_ge(s_bias, 1)
            dve.tensor_tensor(b1f[:, :], ps_cols[:, 2:3], b1c[:, :], ALU.add).then_inc(s_st, 1)
            dve.wait_ge(s_st, 12)
            dve.memset(cols[:, 9:10], 0.0).then_inc(s_wready, 1)

            step(2, 0, 2, [1])
            for g in range(3, HEAD * U):
                step(g, g // U, g % U, stages(g))

            def node_sum(q, ns, lag):
                if live(q.group(lag)):
                    r = q.group(lag)
                    if past(r):
                        dve.wait_ge(ns.cen, r)
                    if lag:
                        dve.wait_ge(ns.uv, q.group(lag - 1))
                        dve.scalar_tensor_tensor(out=res_t[:, :], in0=ps_uv[:, :], scalar=0.0,
                                                 in1=in_t[q.slot(lag)][:, :], op0=ALU.max, op1=ALU.add
                                                 ).then_inc(ns.sum, 1)
                    else:
                        i = q.slot(0)
                        dve.wait_ge(ns.loaded[i], q.turns(0) * 16 + 16)
                        dve.wait_ge(ns.act, q.group(-1))
                        dve.tensor_tensor(res_t[:, :].rearrange("q (j p) -> q j p", j=D),
                                          xt[i][:, :].rearrange("q (p j) -> q j p", j=D),
                                          act_t[:, :].rearrange("q (p j) -> q j p", j=D), ALU.add
                                          ).then_inc(ns.sum, 1)

            def node_norm(q, ns, lag):
                back = lag + 1
                if live(q.group(back + 1)):
                    i = q.slot(back + 1)
                    dve.wait_ge(ns.std, q.group(back))
                    if past(q.group(back + 1)):
                        dve.wait_ge(ns.res, q.group(back + 1))
                    dve.reciprocal(rstd[:, :], std[:, i, :]).then_inc(ns.rstd, 1)
                    dve.wait_ge(ns.rstd, q.group(back))
                    if past(q.turns(back + 1)):
                        dve.wait_ge(ns.stored[i], q.turns(back + 1) * 16)
                    dve.tensor_tensor(res[i][:, :].rearrange("p (r c) -> p r c", c=C),
                                      ps_cen[i][:, :].rearrange("p (r c) -> p r c", c=C),
                                      rstd[:, :].unsqueeze(2).to_broadcast([P, 2 * D, C]), ALU.mult
                                      ).then_inc(ns.res, 1)

            def node_squares(q, ns, lag):
                back = lag + 1
                if live(q.group(back)):
                    i = q.slot(back)
                    dve.wait_ge(ns.sq, q.group(back - 1))
                    if past(q.group(back + 1)):
                        dve.wait_ge(ns.std, q.group(back + 1))
                    dve.tensor_reduce(ssq[:, i, :], sq[:, :].rearrange("p (r c) -> p r c", c=C), AX.X, ALU.add
                                      ).then_inc(ns.ssq, 1)

            def node_step(q, ns, lag):
                node_sum(q, ns, lag)
                node_norm(q, ns, lag)
                node_squares(q, ns, lag)

            def part0(g, it, u, has, nodes=True):
                if not nodes:
                    step(g, it, u, has)
                elif u % 2 == 0:
                    step(g, it, u, has)
                    node_sum(Step(it - NODES_FROM, u // 2 - 1), n0, 0)
                else:
                    q = Step(it - NODES_FROM, u // 2 - 1)
                    step(g, it, u, has, lambda: node_norm(q, n0, 0))
                    node_squares(q, n0, 0)

            def body0(it, nodes=True):
                for u in range(U):
                    part0(it * U + u, it, u, range(DEPTH + 1), nodes)

            with dve.Fori(HEAD, NODES_FROM) as it:
                body0(it, False)
            for it in range(NODES_FROM, NODES_FROM + NODES_HEAD):
                body0(it)
            with dve.Fori(NODES_FROM + NODES_HEAD, BODIES) as it:
                body0(it)
            for g in range(G, G + DEPTH):
                part0(g, g // U, g % U, stages(g))
            for q in node_steps(Q_DRAINED - 1, 0):
                node_step(q, n0, 0)

            dve.wait_ge(n0.clear, K)

            def step1(g, u, build, add):
                if add:
                    starts = window_starts(g - 2)
                    dve.wait_ge(s_sel1, g - 1)
                if build:
                    build_onehot(g, u % 2, rel, s_hot1)
                if add:
                    for s in range(S):
                        add_window(g - 2, s, starts, ps_win[u % 2], s_add1)

            def part1(g, it, u, build, nodes=True):
                q = Step(it - NODES1_FROM, u // 2 - 2)
                if not nodes:
                    step1(g, u, build, True)
                elif u % 2 == 0:
                    step1(g, u, build, True)
                    node_sum(q, n1, 1)
                else:
                    step1(g, u, build, True)
                    node_norm(q, n1, 1)
                    node_squares(q, n1, 1)

            def body1(it, nodes=True):
                for u in range(U):
                    part1(it * U + u, it, u, True, nodes)

            for g in range(U):
                step1(g, g, True, g >= 2)
            with dve.Fori(1, NODES1_FROM) as it:
                body1(it, False)
            for it in range(NODES1_FROM, NODES1_FROM + NODES1_HEAD):
                body1(it)
            with dve.Fori(NODES1_FROM + NODES1_HEAD, BODIES) as it:
                body1(it)
            for g in (G, G + 1):
                part1(g, g // U, g % U, False)
            for q in node_steps(Q1_IN, 1):
                node_step(q, n1, 1)

        @block.tensor
        def _(pe):
            pe.wait_ge(s_pool, 6)

            def step(g, u, has):
                if 1 in has:
                    a, ua = g - 1, (u - 1) % U
                    pe.wait_ge(s_pre, a + 1)
                    if past(a):
                        pe.wait_ge(s_xs, a)
                        pe.wait_ge(s_xd, a)
                    for s in range(S):
                        last = pe.transpose(ps_xt[:, s * P:(s + 1) * P], xx[ua][:, s, :], ident[:, :])
                    last.then_inc(s_t, 1)
                if 4 in has:
                    d, i = g - 4, u % 2
                    pe.wait_ge(s_ms, d + 1)
                    for s in range(S):
                        last = pe.matmul(ps_bt[:, s, :], runmax[i][:, s * P:(s + 1) * P], ident[0:C, 0:C],
                                         start=True, stop=True)
                    last.then_inc(s_bt, 1)
                if 2 in has:
                    b = g - 2
                    pe.wait_ge(s_xs, b + 1)
                    pe.wait_ge(s_xd, b + 1)
                    if past(b):
                        pe.wait_ge(s_relu, b)
                    pe.matmul(ps_h[:, :], wh[:, :], xsxd[(u - 2) % U][:, :], start=True, stop=True).then_inc(s_h, 1)
                if 3 in has:
                    c, i = g - 3, (u - 3) % 2
                    pe.wait_ge(s_relu, c + 1)
                    if past(c):
                        pe.wait_ge(s_btc, c)
                    pe.matmul(ps_m[0:C, :], w2[:, :], hid[i][:, :], start=True, stop=True).then_inc(s_m, 1)
                if 5 in has:
                    e = g - 5
                    pe.wait_ge(s_btc, e + 1)
                    pe.wait_ge(s_hot, e + 1)
                    if past(e - 1):
                        pe.wait_ge(s_add, (e - 1) * S)
                    windows(lambda s: mrow[(u - 5) % 2][:, s, :], onehot[(u - 5) % 2], ps_sel[(u - 5) % 2], s_sel)

            def windows(rows, hot, ps, done):
                for s in range(S):
                    for r in range(2):
                        last = pe.matmul(ps[r * C:(r + 1) * C, s, :], rows(s), hot[:, s, r * MW:(r + 1) * MW],
                                         start=True, stop=True)
                last.then_inc(done, 1)

            step(1, 1, [1])
            pe.wait_ge(s_const, 10)
            pe.wait_ge(s_st, 1)
            pe.matmul(ps_cols[:, 0:1], halves[:, :], mv[:, 0:1], start=True, stop=True).then_inc(s_colp, 1)
            pe.wait_ge(s_st, 5)
            pe.matmul(ps_cols[:, 1:2], halves[:, :], cols[:, 1:2], start=True, stop=True).then_inc(s_colp, 1)
            step(2, 2, [1])
            pe.wait_ge(s_st, 11)
            pe.matmul(ps_cols[:, 2:3], wa[C:P, :], cols[C:P, 6:7], start=True, stop=True).then_inc(s_bias, 1)
            pe.wait_ge(s_wready, 1)

            def node_step(q, ns, lag):
                if live(q.group(lag + 1)):
                    i = q.slot(lag + 1)
                    pe.wait_ge(ns.sum, q.group(lag))
                    if past(q.group(lag + 2)):
                        pe.wait_ge(ns.res, q.group(lag + 2))
                    for j in range(D):
                        last = pe.matmul(ps_cen[i][:, j * P:(j + 1) * P], res_t[:, j * P:(j + 1) * P], cmat[:, :],
                                         start=True, stop=True)
                    last.then_inc(ns.cen, 1)
                if lag and live(q.group(1)):
                    r, i = q.group(1), q.slot(1)
                    pe.wait_ge(ns.copy, q.group(0))
                    pe.wait_ge(s_add1, r * NEED_STEP + NEED)
                    if past(r):
                        pe.wait_ge(ns.sum, r)
                    pe.matmul(ps_uv[:, :], bdu[:, :], in_t[i][:, :], start=True, stop=False)
                    pe.matmul(ps_uv[:, :].rearrange("q (j p) -> q j p", j=D), bdv[:, :],
                              agg[:, bass.ds(r * -DM + (K - 1) * DM, DM)].rearrange("q (p j) -> q j p", j=D),
                              start=False, stop=True).then_inc(ns.uv, 1)
                if lag and live(q.group(0)):
                    i = q.slot(0)
                    pe.wait_ge(ns.loaded[i], q.turns(0) * 16 + 16)
                    if past(q.group(0)):
                        pe.wait_ge(ns.copy, q.group(0))
                    for j in range(D):
                        last = pe.transpose(ps_in[:, j * P:(j + 1) * P], xt[i][:, j * P:(j + 1) * P], ident[:, :])
                    last.then_inc(ns.t, 1)

            def nodes0(h, j):
                node_step(Step(h, j), n0, 0)

            def nodes1(h, j):
                node_step(Step(h, j), n1, 1)

            def no_nodes(h, j):
                pass

            def part0(g, it, u, has, nodes):
                step(g, u, has)
                if u % 2:
                    nodes(it - NODES_FROM, u // 2)

            def body0(it, nodes):
                for u in range(U):
                    part0(it * U + u, it, u, range(DEPTH + 1), nodes)

            step(2, 2, [2])
            for g in range(3, HEAD * U):
                step(g, g % U, stages(g))
            with pe.Fori(HEAD, NODES_FROM) as it:
                body0(it, no_nodes)
            for it in range(NODES_FROM, NODES_FROM + NODES_HEAD):
                body0(it, nodes0)
            with pe.Fori(NODES_FROM + NODES_HEAD, BODIES) as it:
                body0(it, nodes0)
            for g in range(G, G + DEPTH):
                part0(g, g // U, g % U, stages(g), nodes0)
            for q in node_steps(Q_DRAINED, 0):
                node_step(q, n0, 0)

            def step1(g, u, it, reuse):
                pe.wait_ge(s_gather1[u], it * (S * 16) + S * 16)
                pe.wait_ge(s_hot1, g + 1)
                if reuse:
                    pe.wait_ge(s_add1, (g - 1) * S)
                windows(lambda s: xx[u][:, s, 0:C], onehot[u % 2], ps_win[u % 2], s_sel1)

            def body1(it, nodes):
                for u in range(U):
                    step1(it * U + u, u, it, True)
                    if u % 2:
                        nodes(it - NODES1_FROM, u // 2 - 1)

            for g in range(U):
                step1(g, g, 0, g >= 2)
            with pe.Fori(1, NODES1_FROM) as it:
                body1(it, no_nodes)
            pe.wait_ge(s_wu, 64)
            for it in range(NODES1_FROM, NODES1_FROM + NODES1_HEAD):
                body1(it, nodes1)
            with pe.Fori(NODES1_FROM + NODES1_HEAD, BODIES) as it:
                body1(it, nodes1)
            for q in node_steps(Q1_IN, 1):
                node_step(q, n1, 1)


def kernel(x, src, dst, L0_gnn_gamma, L0_gnn_beta, L0_gnn_W1, L0_gnn_b1, L0_gnn_W2, L0_gnn_b2, L1_gnn_U, L1_gnn_V):
    import numpy as np
    import concourse.bacc as bacc
    from concourse.bass_utils import run_bass_kernel_spmd

    def padded(a, before, count, fill):
        full = np.concatenate([np.full((1,), fill, a.dtype), a, np.full((count + 2 - a.shape[0],), fill, a.dtype)])
        return full[1 - before:1 - before + count]

    def columns(a, tiles):
        return np.ascontiguousarray(a.reshape(tiles, P).T)

    x = np.asarray(x)
    x_padded = np.concatenate([x, np.zeros((NP - N, C), x.dtype)])
    src_r = np.asarray(src)[::-1]
    dst_r = np.asarray(dst)[::-1]
    arrays = {
        "x": x_padded,
        "x_pairs": x_padded.reshape(MP, 2 * C).T,
        "src_cols": columns(padded(src_r, 0, IDX_COLS * P, 0), IDX_COLS),
        "dst_cols": columns(padded(dst_r, 0, EP, -1), T),
        "dst_prev_cols": columns(padded(dst_r, 1, EP, -1), T),
        "dst_next_cols": columns(padded(dst_r, -1, EP, -1), T),
        "dst_rows": padded(dst_r, 0, EP, -1).reshape(P, EP // P),
        "dst_prev_rows": padded(dst_r, 1, EP, -1).reshape(P, EP // P),
        "dst_low": padded(dst_r, 0, EP, -1)[P - 1::P].reshape(1, T),
        "gamma": np.asarray(L0_gnn_gamma).reshape(C, 1),
        "beta": np.asarray(L0_gnn_beta).reshape(C, 1),
        "W1": np.asarray(L0_gnn_W1),
        "b1": np.asarray(L0_gnn_b1).reshape(HID, 1),
        "W2": np.asarray(L0_gnn_W2),
        "b2": np.asarray(L0_gnn_b2).reshape(C, 1),
        "U_t": np.asarray(L1_gnn_U).T,
        "V_t": np.asarray(L1_gnn_V).T,
    }
    nc = bacc.Bacc("TRN2", target_bir_lowering=False, num_devices=1)
    ins, args = {}, []
    for name, a in arrays.items():
        a = np.ascontiguousarray(a)
        ins[f"in_{name}"] = a
        args.append(nc.dram_tensor(f"in_{name}", a.shape, mybir.dt.from_np(a.dtype), kind="ExternalInput").ap())
    out = nc.dram_tensor("out", (NP, C), F32, kind="ExternalOutput").ap()
    gnn_kernel(nc, *args, out)
    r = run_bass_kernel_spmd(nc, [ins], core_ids=[0])
    return r.results[0]["out"][:N]
```
